# Optimizing a Trainium2 kernel written in Bass

```python
import numpy as np
import jax
import jax.numpy as jnp

def _softmax(x, axis=-1):
    return jax.nn.softmax(x, axis=axis)

def _gelu(x):
    return jax.nn.gelu(x, approximate=True)

def _silu(x):
    return jax.nn.silu(x)

def _sigmoid(x):
    return jax.nn.sigmoid(x)

def _layernorm(x, axis=-1, eps=1e-05):
    m = jnp.mean(x, axis=axis, keepdims=True)
    v = jnp.var(x, axis=axis, keepdims=True)
    return (x - m) / jnp.sqrt(v + eps)

def _scatter_add(tgt, idx, src, axis=0):
    return tgt.at[idx].add(src)

def _segment_sum(src, seg, n):
    return jax.ops.segment_sum(src, seg, n)
kernel_name = 'mk_sandwich_d1_jaxref_r8_28a12d'

def setup_inputs(seed: int=0):
    np.random.seed(seed)
    _w = jnp.asarray

    def _L0_attn_setup():
        import jax, jax.numpy as jnp
        import numpy as np
        import math
        D_MODEL, D_STATE, D_CONV = (128, 16, 4)
        D_INNER = 2 * D_MODEL
        DT_RANK = math.ceil(D_MODEL / 16)
        B, L = (4, 256)

        def _layernorm(x, g, b, eps=1e-05):
            m = jnp.mean(x, axis=-1, keepdims=True)
            v = jnp.mean(jnp.square(x - m), axis=-1, keepdims=True)
            return (x - m) * jax.lax.rsqrt(v + eps) * g + b

        def _mamba(xn, W_in, conv_w, conv_b, W_xp, W_dt, dt_bias, A_log, D_skip, W_out):
            xz = xn @ W_in
            xi, z = jnp.split(xz, 2, axis=-1)
            xi_t = jnp.transpose(xi, (0, 2, 1))
            xc = jax.lax.conv_general_dilated(xi_t, conv_w, window_strides=(1,), padding=[(D_CONV - 1, 0)], feature_group_count=D_INNER, dimension_numbers=('NCH', 'OIH', 'NCH'))
            xc = jnp.transpose(xc, (0, 2, 1)) + conv_b
            xc = jax.nn.silu(xc)
            x_dbl = xc @ W_xp
            dt_lo, Bm, Cm = jnp.split(x_dbl, [DT_RANK, DT_RANK + D_STATE], axis=-1)
            delta = jax.nn.softplus(dt_lo @ W_dt + dt_bias)
            A = -jnp.exp(A_log)

            def step(h, inp):
                dt_t, B_t, C_t, u_t = inp
                dA = jnp.exp(dt_t[..., None] * A)
                h = h * dA + (dt_t * u_t)[..., None] * B_t[:, None, :]
                y = jnp.einsum('bdn,bn->bd', h, C_t)
                return (h, y)
            h0 = jnp.zeros((xn.shape[0], D_INNER, D_STATE), xn.dtype)
            inputs = (jnp.transpose(delta, (1, 0, 2)), jnp.transpose(Bm, (1, 0, 2)), jnp.transpose(Cm, (1, 0, 2)), jnp.transpose(xc, (1, 0, 2)))
            _, ys = jax.lax.scan(step, h0, inputs)
            y = jnp.transpose(ys, (1, 0, 2)) + xc * D_skip
            y = y * jax.nn.silu(z)
            return y @ W_out
        key = jax.random.key(seed)
        ks = jax.random.split(key, 10)
        s = 0.02
        x = jax.random.normal(ks[0], (B, L, D_MODEL), dtype=jnp.float32)
        ln_g = jnp.ones((D_MODEL,), jnp.float32)
        ln_b = jnp.zeros((D_MODEL,), jnp.float32)
        W_in = jax.random.normal(ks[1], (D_MODEL, 2 * D_INNER), jnp.float32) * s
        conv_w = jax.random.normal(ks[2], (D_INNER, 1, D_CONV), jnp.float32) * s
        conv_b = jnp.zeros((D_INNER,), jnp.float32)
        W_xp = jax.random.normal(ks[3], (D_INNER, DT_RANK + 2 * D_STATE), jnp.float32) * s
        W_dt = jax.random.normal(ks[4], (DT_RANK, D_INNER), jnp.float32) * DT_RANK ** (-0.5)
        dt_bias = jnp.full((D_INNER,), float(np.log(np.expm1(0.01))), jnp.float32)
        A_log = jnp.log(jnp.broadcast_to(jnp.arange(1, D_STATE + 1, dtype=jnp.float32), (D_INNER, D_STATE)))
        D_skip = jnp.ones((D_INNER,), jnp.float32)
        W_out = jax.random.normal(ks[5], (D_INNER, D_MODEL), jnp.float32) * s
        return dict(x=x, ln_g=ln_g, ln_b=ln_b, W_in=W_in, conv_w=conv_w, conv_b=conv_b, W_xp=W_xp, W_dt=W_dt, dt_bias=dt_bias, A_log=A_log, D_skip=D_skip, W_out=W_out)
    _L0_attn_in = _L0_attn_setup()

    def _L0_ffn_setup():
        import jax, jax.numpy as jnp
        import numpy as np
        N_EMBD = 128
        NUM_EXPERTS = 8
        TOP_K = 2
        D_FF = 4 * N_EMBD
        B, S = (4, 256)
        key = jax.random.key(seed)
        ks = jax.random.split(key, 7)
        scale = lambda fan_in: 1.0 / np.sqrt(fan_in)
        x = jax.random.normal(ks[0], (B, S, N_EMBD), dtype=jnp.float32)
        W_router = jax.random.normal(ks[1], (N_EMBD, NUM_EXPERTS), dtype=jnp.float32) * scale(N_EMBD)
        b_router = jnp.zeros((NUM_EXPERTS,), dtype=jnp.float32)
        W1 = jax.random.normal(ks[2], (NUM_EXPERTS, N_EMBD, D_FF), dtype=jnp.float32) * scale(N_EMBD)
        b1 = jnp.zeros((NUM_EXPERTS, D_FF), dtype=jnp.float32)
        W2 = jax.random.normal(ks[3], (NUM_EXPERTS, D_FF, N_EMBD), dtype=jnp.float32) * scale(D_FF)
        b2 = jnpp = jnp.zeros((NUM_EXPERTS, N_EMBD), dtype=jnp.float32)
        return {'x': x, 'W_router': W_router, 'b_router': b_router, 'W1': W1, 'b1': b1, 'W2': W2, 'b2': b2}
    _L0_ffn_in = _L0_ffn_setup()
    _d = {'L0_attn_x': _L0_attn_in['x'], 'L0_attn_ln_g': _L0_attn_in['ln_g'], 'L0_attn_ln_b': _L0_attn_in['ln_b'], 'L0_attn_W_in': _L0_attn_in['W_in'], 'L0_attn_conv_w': _L0_attn_in['conv_w'], 'L0_attn_conv_b': _L0_attn_in['conv_b'], 'L0_attn_W_xp': _L0_attn_in['W_xp'], 'L0_attn_W_dt': _L0_attn_in['W_dt'], 'L0_attn_dt_bias': _L0_attn_in['dt_bias'], 'L0_attn_A_log': _L0_attn_in['A_log'], 'L0_attn_D_skip': _L0_attn_in['D_skip'], 'L0_attn_W_out': _L0_attn_in['W_out'], 'L0_ffn_W_router': _L0_ffn_in['W_router'], 'L0_ffn_b_router': _L0_ffn_in['b_router'], 'L0_ffn_W1': _L0_ffn_in['W1'], 'L0_ffn_b1': _L0_ffn_in['b1'], 'L0_ffn_W2': _L0_ffn_in['W2'], 'L0_ffn_b2': _L0_ffn_in['b2']}
    _x0 = _d['L0_attn_x']
    _d['L0_attn_x'] = jax.random.normal(jax.random.fold_in(jax.random.key(seed), 1), (8, 512, 128), dtype=_x0.dtype)
    del _x0
    return _d

def reference(L0_attn_x, L0_attn_ln_g, L0_attn_ln_b, L0_attn_W_in, L0_attn_conv_w, L0_attn_conv_b, L0_attn_W_xp, L0_attn_W_dt, L0_attn_dt_bias, L0_attn_A_log, L0_attn_D_skip, L0_attn_W_out, L0_ffn_W_router, L0_ffn_b_router, L0_ffn_W1, L0_ffn_b1, L0_ffn_W2, L0_ffn_b2):

    def _L0_attn_ref(x, ln_g, ln_b, W_in, conv_w, conv_b, W_xp, W_dt, dt_bias, A_log, D_skip, W_out):
        import jax, jax.numpy as jnp
        import numpy as np
        import math
        D_MODEL, D_STATE, D_CONV = (128, 16, 4)
        D_INNER = 2 * D_MODEL
        DT_RANK = math.ceil(D_MODEL / 16)
        B, L = (4, 256)

        def _layernorm(x, g, b, eps=1e-05):
            m = jnp.mean(x, axis=-1, keepdims=True)
            v = jnp.mean(jnp.square(x - m), axis=-1, keepdims=True)
            return (x - m) * jax.lax.rsqrt(v + eps) * g + b

        def _mamba(xn, W_in, conv_w, conv_b, W_xp, W_dt, dt_bias, A_log, D_skip, W_out):
            xz = xn @ W_in
            xi, z = jnp.split(xz, 2, axis=-1)
            xi_t = jnp.transpose(xi, (0, 2, 1))
            xc = jax.lax.conv_general_dilated(xi_t, conv_w, window_strides=(1,), padding=[(D_CONV - 1, 0)], feature_group_count=D_INNER, dimension_numbers=('NCH', 'OIH', 'NCH'))
            xc = jnp.transpose(xc, (0, 2, 1)) + conv_b
            xc = jax.nn.silu(xc)
            x_dbl = xc @ W_xp
            dt_lo, Bm, Cm = jnp.split(x_dbl, [DT_RANK, DT_RANK + D_STATE], axis=-1)
            delta = jax.nn.softplus(dt_lo @ W_dt + dt_bias)
            A = -jnp.exp(A_log)

            def step(h, inp):
                dt_t, B_t, C_t, u_t = inp
                dA = jnp.exp(dt_t[..., None] * A)
                h = h * dA + (dt_t * u_t)[..., None] * B_t[:, None, :]
                y = jnp.einsum('bdn,bn->bd', h, C_t)
                return (h, y)
            h0 = jnp.zeros((xn.shape[0], D_INNER, D_STATE), xn.dtype)
            inputs = (jnp.transpose(delta, (1, 0, 2)), jnp.transpose(Bm, (1, 0, 2)), jnp.transpose(Cm, (1, 0, 2)), jnp.transpose(xc, (1, 0, 2)))
            _, ys = jax.lax.scan(step, h0, inputs)
            y = jnp.transpose(ys, (1, 0, 2)) + xc * D_skip
            y = y * jax.nn.silu(z)
            return y @ W_out
        xn = _layernorm(x, ln_g, ln_b)
        return _mamba(xn, W_in, conv_w, conv_b, W_xp, W_dt, dt_bias, A_log, D_skip, W_out) + x

    def _L0_ffn_ref(x, W_router, b_router, W1, b1, W2, b2):
        import jax, jax.numpy as jnp
        import numpy as np
        N_EMBD = 128
        NUM_EXPERTS = 8
        TOP_K = 2
        D_FF = 4 * N_EMBD
        B, S = (4, 256)
        Bv, Sv, D = x.shape
        flat_x = x.reshape(-1, D)
        T = flat_x.shape[0]
        logits = flat_x @ W_router + b_router
        top_vals, top_idx = jax.lax.top_k(logits, TOP_K)
        neg_inf = jnp.full_like(logits, -jnp.inf)
        sparse_logits = neg_inf.at[jnp.arange(T)[:, None], top_idx].set(top_vals)
        router_weights = jax.nn.softmax(sparse_logits, axis=-1)
        final_output = jnp.zeros_like(flat_x)
        for e in range(NUM_EXPERTS):
            expert_mask = jnp.any(top_idx == e, axis=-1)
            h = jax.nn.relu(flat_x @ W1[e] + b1[e])
            y = h @ W2[e] + b2[e]
            w = router_weights[:, e] * expert_mask.astype(x.dtype)
            final_output = final_output + y * w[:, None]
        return final_output.reshape(Bv, Sv, D)
    x = L0_attn_x
    x = x + _layernorm(_L0_attn_ref(_layernorm(x, axis=-1), L0_attn_ln_g, L0_attn_ln_b, L0_attn_W_in, L0_attn_conv_w, L0_attn_conv_b, L0_attn_W_xp, L0_attn_W_dt, L0_attn_dt_bias, L0_attn_A_log, L0_attn_D_skip, L0_attn_W_out), axis=-1)
    x = x + _layernorm(_L0_ffn_ref(_layernorm(x, axis=-1), L0_ffn_W_router, L0_ffn_b_router, L0_ffn_W1, L0_ffn_b1, L0_ffn_W2, L0_ffn_b2), axis=-1)
    return x

_drawn_inputs = setup_inputs


def setup_inputs(seed=0):
    import zlib

    import numpy as np

    out = dict(_drawn_inputs(seed))
    spreads = {'L0_attn_ln_g': (1.0, 0.6),
     'L0_attn_ln_b': (0.0, 0.8),
     'L0_attn_conv_b': (0.0, 0.694),
     'L0_attn_dt_bias': (-4.600165843963623, 0.6),
     'L0_attn_D_skip': (1.0, 0.6),
     'L0_ffn_b_router': (0.0, 0.1),
     'L0_ffn_b1': (0.0, 0.1),
     'L0_ffn_b2': (0.0, 0.1)}
    factors = {'L0_attn_W_in': 6.438,
     'L0_attn_conv_w': 8.0,
     'L0_attn_W_xp': 8.0,
     'L0_attn_W_dt': 8.0,
     'L0_attn_A_log': 8.0,
     'L0_attn_W_out': 6.721}
    for name, (base, spread) in spreads.items():
        noise = np.random.default_rng([zlib.crc32(name.encode()), seed]).standard_normal(out[name].shape)
        drawn = base * np.exp(spread * noise) if base else spread * noise
        out[name] = jnp.asarray(drawn.astype(out[name].dtype))
    for name, factor in factors.items():
        out[name] = (out[name] * factor).astype(out[name].dtype)
    return out
```

```python
from contextlib import ExitStack

import concourse.bass as bass
from concourse import mybir

F32 = mybir.dt.float32
U32 = mybir.dt.uint32
I32 = mybir.dt.int32
ALU = mybir.AluOpType
ACT = mybir.ActivationFunctionType
AX = mybir.AxisListType

P = 128
EPS = 1e-5
L1P_A, L1P_K, L1P_KB = 0.24810788804420705, 0.3753309023989405, 0.19728378793895784
L1P_D, L1P_E = 0.25123911755073414, 0.9514290285127261
EXP_LN_TABLES = "natural_log_exp_and_others"


def reach(eng, *waits):
    waits = [(sem, count) for sem, count in waits if not (isinstance(count, int) and count <= 0)]
    for _, count in waits:
        if not isinstance(count, int):
            eng.compute_val(count)
    for sem, count in waits:
        eng.wait_ge(sem, count)


def mamba_moe_kernel(nc, x, ln_g, ln_b, W_in, conv_w, conv_b, W_xp, W_dt, dt_bias, A_log, D_skip,
                     W_out, W_router, b_router, W1, b1, W2, b2, out):
    NBATCH, T, D = x.shape
    DI = D_skip.shape[0]
    NST = A_log.shape[1]
    TAPS = conv_w.shape[2]
    RANK = W_dt.shape[0]
    E, _, DF = W1.shape
    assert D == P and T == 512 and DI == 2 * P and E == 8 and P % NST == 0
    NT = T // P
    NH = DI // P
    CG = P // NST
    NG = DI // CG
    NP = NG // 2
    GQ = 32 // CG
    FC = DF // P
    UN = E * FC
    LAG = 5
    RING, PRE = 8, 4
    SS = NG
    NEW0 = 10
    SPLIT = 24
    RT = 10
    NPA, NPC = 8, 5

    ctx = ExitStack()
    with ctx:
        def sb(name, shape, dt=F32):
            return ctx.enter_context(nc.sbuf_tensor(name, shape, dt))

        def ps(name, shape):
            return ctx.enter_context(nc.psum_tensor(name, shape, F32))

        def sem(name):
            return ctx.enter_context(nc.semaphore(name))

        NROW = NG + UN + 3 * NH + 2
        rows = sb("rows", [P, P])
        cols = sb("cols", [P, NROW])
        Amat = sb("Amat", [P, NG])
        win = sb("win", [P, 2 * DI])
        cwb = sb("cwb", [P, DI * TAPS])
        wconv = sb("wconv", [P, TAPS, DI])
        wxp = sb("wxp", [P, NH, RANK + 2 * NST])
        wdt = sb("wdt", [RANK, DI])
        wout = sb("wout", [P, NH, D])
        wrt = sb("wrt", [P, E])
        brb = sb("brb", [P, E])
        w1 = sb("w1", [P, E, DF])
        w2 = sb("w2", [P, E, FC, D])
        b2s = sb("b2s", [E, D])
        ident = sb("ident", [P, P])
        sel = sb("sel", [P, GQ, 32])
        iota_i = sb("iota_i", [P, E], I32)
        iota_f = sb("iota_f", [P, E])
        B1C = NG
        CBC, DTC, DSC, GC, BC = (B1C + UN + k for k in (0, NH, 2 * NH, 3 * NH, 3 * NH + 1))

        xa = sb("xa", [P, NT, D])
        xha = sb("xha", [P, NT, D])
        xn = sb("xn", [P, NT, D])
        xnT = sb("xnT", [P, TAPS - 1 + T])
        uza = sb("uza", [P, 2 * NH, T])
        NX = RANK + 2 * NST
        xd = sb("xd", [NX, T])
        delta = sb("delta", [P, NH, T])
        du = sb("du", [P, NH, T])
        st = sb("st", [P, NT, 6])
        mv = sb("mv", [P, NT, 2])
        rs = sb("rs", [P, NT])
        rq = sb("rq", [P, 2, NT])
        rs2 = sb("rs2", [P, NT])
        bcc = sb("bcc", [P, 2, T])
        dring = sb("dring", [P, RING, 2, T])
        uring = sb("uring", [P, RING, 2, T])
        uzc = sb("uzc", [P, 2 * NH, T])
        xc = sb("xc", [P, NT, D])
        xhc = sb("xhc", [P, NT, D])
        yg = sb("yg", [P, NH, T])
        r1 = sb("r1", [P, NT, D])
        x1 = sb("x1", [P, NT, D])
        xfT = sb("xfT", [P, T])
        stc = sb("stc", [P, NT, 6])
        mvc = sb("mvc", [P, NT, 2])
        rsc = sb("rsc", [P, NT])
        sto = sb("sto", [P, NT, 6])
        mvo = sb("mvo", [P, NT, 2])
        rso = sb("rso", [P, NT])
        fence = sb("fence", [P, 1])
        csts = sb("csts", [P, 4])
        sp1 = sb("sp1", [P, NH, T])
        sp2 = sb("sp2", [P, NH, T])
        lg = sb("lg", [P, NT, E])
        mx = sb("mx", [P, NT, E])
        ix = sb("ix", [P, NT, E], U32)
        ixf = sb("ixf", [P, NT, 2])
        m1 = sb("m1", [P, NT, E])
        m2 = sb("m2", [P, NT, E])
        ex = sb("ex", [P, NT, E])
        sm = sb("sm", [P, NT])
        wr = sb("wr", [P, NT, E])
        wrT = sb("wrT", [E, T])
        hb = sb("hb", [P, 2, FC, T])
        acc = sb("acc", [P, NT, D])
        x1e = sb("x1e", [P, NT, D])
        xo = sb("xo", [P, NT, D])

        xd_dram = nc.dram_tensor("xd_dram", [NBATCH, NX, T], F32, kind="Internal").ap()
        xh_dram = nc.dram_tensor("xh_dram", [NBATCH, P, NT * D], F32, kind="Internal").ap()

        ypsum = ps("ypsum", [P, NH, T])
        hpsum = ps("hpsum", [P, 2, T])
        opsum = ps("opsum", [P, 2, T])
        work = ps("work", [P, 2, T])

        rows_loaded, proj_loaded, ffn_loaded = sem("rows_loaded"), sem("proj_loaded"), sem("ffn_loaded")
        const_made, cols_turned, cols_copied, a_exp = (sem("const_made"), sem("cols_turned"),
                                                       sem("cols_copied"), sem("a_exp"))
        a_made, w_folded, pads_made = sem("a_made"), sem("w_folded"), sem("pads_made")
        x_loaded, xc_loaded, uz_copied = sem("x_loaded"), sem("xc_loaded"), sem("uz_copied")
        b_loaded, c_loaded, x1_copied = sem("b_loaded"), sem("c_loaded"), sem("x1_copied")
        xd_stored, xh_stored = sem("xd_stored"), sem("xh_stored")
        out_stored = sem("out_stored")
        delta_spread = [sem(f"delta_spread{r}") for r in range(RING)]
        du_spread = [sem(f"du_spread{r}") for r in range(RING)]
        norm_a, xh_ready = sem("norm_a"), sem("xh_ready")
        db_done, scan_done, y_skip = sem("db_done"), sem("scan_done"), sem("y_skip")
        norm_c, r1_ready, x1_ready, xf_ready = (sem("norm_c"), sem("r1_ready"), sem("x1_ready"),
                                                sem("xf_ready"))
        route, w_ready, b2_added = sem("route"), sem("w_ready"), sem("b2_added")
        acc_done, norm_o, out_ready = sem("acc_done"), sem("norm_o"), sem("out_ready")
        rs_ready, rsc_ready, rso_ready = sem("rs_ready"), sem("rsc_ready"), sem("rso_ready")
        xn_ready, pa_read, silu_done = sem("xn_ready"), sem("pa_read"), sem("silu_done")
        lp_ready = sem("lp_ready")
        soft, exp_done = sem("soft"), sem("exp_done")
        xfT_ready, route_exp, wrT_ready = sem("xfT_ready"), sem("route_exp"), sem("wrT_ready")
        relu_done = sem("relu_done")
        hc_done, delta_ready, du_ready, gated = (sem("hc_done"), sem("delta_ready"), sem("du_ready"),
                                                 sem("gated"))
        summed, pa_filled, pc_filled = sem("summed"), sem("pa_filled"), sem("pc_filled")
        h_filled, o_filled = sem("h_filled"), sem("o_filled")

        def over_batches(eng, iteration):
            def flags(it):
                return dict(ahead=it + 1 < NBATCH, scan=0 <= it < NBATCH, post=0 <= it - 1 < NBATCH,
                            late=0 <= it - 2 < NBATCH)
            for it in (-1, 0, 1):
                iteration(it, **flags(it))
            with eng.Fori(2, NBATCH - 1) as it:
                iteration(it, ahead=True, scan=True, post=True, late=True)
            for it in (NBATCH - 1, NBATCH, NBATCH + 1):
                iteration(it, **flags(it))

        def new_units(s):
            n = s - NEW0
            return [2 * n, 2 * n + 1] if 0 <= n < 2 else [n + 2] if n >= 2 else []

        def old_units(s):
            cut = [24, 26, 28, 29, 31, 33, 35, 37]
            return list(range(cut[s], cut[s + 1])) if s + 1 < len(cut) else []
        assert SS - NEW0 + 2 == SPLIT and UN + LAG == 37

        block = ctx.enter_context(nc.Block())

        @block.sync
        def _(sp):
            sp.dma_start(rows[0:NG, :], A_log.rearrange("(g c) n -> g (c n)", c=CG)).then_inc(rows_loaded, 16)
            sp.dma_start(rows[B1C:B1C + UN, :], b1.rearrange("e (f p) -> (e f) p", p=P)).then_inc(rows_loaded, 16)
            for at, v in ((CBC, conv_b), (DTC, dt_bias), (DSC, D_skip), (GC, ln_g), (BC, ln_b)):
                k = v.shape[0] // P
                sp.dma_start(rows[at:at + k, :], v.rearrange("(h p) -> h p", p=P)).then_inc(rows_loaded, 16)
            sp.dma_start(xa[:, :, :], x[0].rearrange("(i p) d -> p i d", p=P)).then_inc(x_loaded, 16)
            sp.dma_start(win[:, :], W_in).then_inc(proj_loaded, 16)
            sp.dma_start(cwb[:, :], conv_w.rearrange("c a k -> (c a k)").partition_broadcast(P)).then_inc(proj_loaded, 16)
            sp.dma_start(wxp[:, :, :], W_xp.rearrange("(h p) n -> p h n", p=P)).then_inc(proj_loaded, 16)
            sp.dma_start(wdt[:, :], W_dt).then_inc(proj_loaded, 16)
            sp.dma_start(wout[:, :, :], W_out.rearrange("(h p) n -> p h n", p=P)).then_inc(ffn_loaded, 16)
            sp.dma_start(wrt[:, :], W_router).then_inc(ffn_loaded, 16)
            sp.dma_start(brb[:, :], b_router.partition_broadcast(P)).then_inc(ffn_loaded, 16)
            sp.dma_start(b2s[:, :], b2).then_inc(ffn_loaded, 16)
            for e in range(E):
                sp.dma_start(w1[:, e, :], W1[e]).then_inc(ffn_loaded, 16)
                sp.dma_start(w2[:, e, :, :], W2[e].rearrange("(f p) n -> p f n", p=P)).then_inc(ffn_loaded, 16)

            def spread(it, j):
                pair = NP * it + j
                made = [(du_ready, NH * it + j // (NP // NH) + 1)] if j % (NP // NH) == 0 else []
                reach(sp, *made, (summed, pair - RING + 1))
                for i in range(2):
                    g = 2 * j + i
                    c0 = (g * CG) % P
                    for src, ring, n, loaded in ((delta, dring, RING, delta_spread), (du, uring, RING, du_spread)):
                        rowsrc = src[c0:c0 + CG, g * CG // P, :].unsqueeze(1).broadcast_to([CG, NST, T])
                        sp.dma_start(ring[:, j % n, i, :], rowsrc).then_inc(loaded[j % n], 16)

            def iteration(it, ahead, scan, post, late):
                if ahead and not (isinstance(it, int) and it < 0):
                    sp.wait_ge(xh_ready, it + 1)
                    sp.dma_start(xa[:, :, :], x[bass.ds(it + 1, 1)].rearrange("a (i p) d -> p (a i) d", p=P)
                                 ).then_inc(x_loaded, 16)
                if scan:
                    for k, (used, loaded) in enumerate(((db_done, b_loaded), (hc_done, c_loaded))):
                        reach(sp, *([] if k else [(xd_stored, 16 * (it + 1))]), (used, NP * it))
                        n0 = RANK + k * NST
                        sp.dma_start(bcc[:, k, :], xd_dram[bass.ds(it, 1), n0:n0 + NST, :].broadcast_to([CG, NST, T])
                                     ).then_inc(loaded, 16)
                    spread(it, 4)
                    spread(it, 5)
                    reach(sp, (gated, NH * it))
                    sp.dma_start(uzc[:, :, :], uza[:, :, :]).then_inc(uz_copied, 16)
                if ahead:
                    sp.wait_ge(xh_ready, it + 2)
                    sp.dma_start(xh_dram[bass.ds(it + 1, 1)].rearrange("a p n -> p (a n)"),
                                 xha[:, :, :].rearrange("p i d -> p (i d)")).then_inc(xh_stored, 16)
                if scan:
                    spread(it, 6)
                    spread(it, 7)
                    reach(sp, (x1_ready, it))
                    sp.wait_ge(xh_stored, 16 * (it + 1))
                    sp.dma_start(xc[:, :, :], x[bass.ds(it, 1)].rearrange("a (i p) d -> p (a i) d", p=P)
                                 ).then_inc(xc_loaded, 16)
                    sp.dma_start(xhc[:, :, :].rearrange("p i d -> p (i d)"),
                                 xh_dram[bass.ds(it, 1)].rearrange("a p n -> p (a n)")).then_inc(xc_loaded, 16)
                    for j in range(8, 11):
                        spread(it, j)
                if late:
                    sp.wait_ge(out_ready, it - 1)
                    sp.dma_start(out[bass.ds(it - 2, 1)].rearrange("a (i p) d -> p (a i) d", p=P), xo[:, :, :]
                                 ).then_inc(out_stored, 16)
                    sp.wait_ge(out_stored, 16 * (it - 1))
                if post:
                    sp.wait_ge(x1_ready, it)
                    sp.dma_start(x1e[:, :, :], x1[:, :, :]).then_inc(x1_copied, 16)
                if scan:
                    for j in range(11, NP):
                        spread(it, j)
                if ahead:
                    sp.wait_ge(pa_read, NPA * (it + 1) + 6)
                    sp.dma_start(xd_dram[bass.ds(it + 1, 1)].rearrange("a n t -> n (a t)"), xd[:, :]).then_inc(xd_stored, 16)
                    for j in range(PRE):
                        spread(it + 1, j)

            over_batches(sp, iteration)
            sp.wait_ge(out_stored, 16 * NBATCH)
            sp.wait_ge(xd_stored, 16 * NBATCH)
            sp.wait_ge(xh_stored, 16 * NBATCH)

        @block.gpsimd
        def _(pool):
            pool.memset(ident[:, :], 0.0).then_inc(const_made, 1)
            pool.memset(sel[:, :, :], 1.0).then_inc(const_made, 1)
            pool.iota(iota_i[:, :], [[1, E]], base=0, channel_multiplier=0).then_inc(const_made, 1)
            pool.wait_ge(const_made, 3)
            pool.affine_select(out=ident[:, :], in_=ident[:, :], compare_op=ALU.not_equal, fill=1.0, base=0,
                               pattern=[[-1, P]], channel_multiplier=1).then_inc(const_made, 1)
            pool.affine_select(out=sel[:, :, :], in_=sel[:, :, :], compare_op=ALU.is_ge, fill=0.0, base=0,
                               pattern=[[P, GQ], [-NST, 32]], channel_multiplier=1).then_inc(const_made, 1)
            pool.wait_ge(const_made, 5)
            pool.affine_select(out=sel[:, :, :], in_=sel[:, :, :], compare_op=ALU.is_ge, fill=0.0, base=NST - 1,
                               pattern=[[-P, GQ], [NST, 32]], channel_multiplier=-1).then_inc(const_made, 1)

            def states_to_output(it, j):
                if j == 0:
                    pool.wait_ge(c_loaded, 16 * (it + 1))
                pool.wait_ge(scan_done, NP * it + j + 1)
                h = uring[:, j % RING, :, :]
                c = bcc[:, 1, :].unsqueeze(1).broadcast_to([P, 2, T])
                pool.tensor_tensor(h, h, c, ALU.mult).then_inc(hc_done, 1)

            def gate(b, h):
                pool.wait_ge(y_skip, NH * b + h + 1)
                pool.tensor_tensor(yg[:, h, :], yg[:, h, :], uzc[:, NH + h, :], ALU.mult).then_inc(gated, 1)

            def steps_of_time(b, h):
                pool.wait_ge(delta_ready, NH * b + h + 1)
                pool.wait_ge(silu_done, b + 1)
                pool.tensor_tensor(du[:, h, :], delta[:, h, :], uza[:, h, :], ALU.mult).then_inc(du_ready, 1)

            def iteration(it, ahead, scan, post, late):
                for s in range(SS):
                    if s == 0 and post:
                        states_to_output(it - 1, NP - 1)
                    if s == 3 and post:
                        gate(it - 1, 1)
                    if s >= 2 and s % 2 == 0 and scan:
                        states_to_output(it, s // 2 - 1)
                    if s == 20 and scan:
                        gate(it, 0)
                    if s in (23, 26) and ahead:
                        steps_of_time(it + 1, (s - 23) // 3)

            over_batches(pool, iteration)

        @block.scalar
        def _(act):
            act.preload_act_table_set(EXP_LN_TABLES)
            act.wait_ge(cols_turned, 1)
            act.activation(cols[:, :], work[:, 0, 0:NROW], ACT.Copy).then_inc(cols_copied, 1)
            act.wait_ge(cols_copied, 1)
            act.activation(Amat[:, :], cols[:, 0:NG], ACT.Exp).then_inc(a_exp, 1)

            def decay(it, g):
                j, i = g // 2, g % 2
                if isinstance(it, int) and it == 0 and g == 0:
                    act.wait_ge(a_made, 1)
                if i == 0:
                    act.wait_ge(delta_spread[j % RING], 32 * ((NP // RING) * it + j // RING + 1))
                act.activation(dring[:, j % RING, i, :], dring[:, j % RING, i, :], ACT.Exp,
                               scale=Amat[:, g:g + 1]).then_inc(exp_done, 1)

            def read_proj(b, k, dst, src, func, **affine):
                act.wait_ge(pa_filled, NPA * b + k + 1)
                act.activation(dst, src, func, **affine).then_inc(pa_read, 1)

            def relu(b, u):
                e, f = u // FC, u % FC
                act.wait_ge(h_filled, UN * b + u + 1)
                if f == 0:
                    reach(act, (o_filled, UN * b + FC * (e - 1)))
                act.activation(hb[:, e % 2, f, :], hpsum[:, u % 2, :], ACT.Relu,
                               bias=cols[:, B1C + u:B1C + u + 1]).then_inc(relu_done, 1)

            def inverse_deviation(dst, var, ready, count):
                act.activation(dst[:, :], var, ACT.Ln, bias=csts[:, 0:1]).then_inc(ready, 1)
                act.wait_ge(ready, count - 1)
                act.activation(dst[:, :], dst[:, :], ACT.Exp, scale=-0.5).then_inc(ready, 1)

            def iteration(it, ahead, scan, post, late):
                for s in range(SS):
                    if scan and s + 2 < NG:
                        decay(it, s + 2)
                    if ahead and s + 2 >= NG:
                        decay(it + 1, s + 2 - NG)
                    if late:
                        for k in old_units(s):
                            if k < UN:
                                relu(it - 2, k)
                        if s == 8:
                            act.wait_ge(norm_o, 3 * (it - 2) + 2)
                            inverse_deviation(rso, mvo[:, :, 1], rso_ready, 2 * (it - 2) + 2)
                    if post:
                        b = it - 1
                        if s in (6, 7):
                            act.wait_ge(norm_c, 5 * b + (2, 5)[s - 6])
                            inverse_deviation(rsc, mvc[:, :, 1], rsc_ready, 4 * b + (2, 4)[s - 6])
                        if s == 9:
                            act.wait_ge(pc_filled, NPC * b + 2)
                            act.activation(xfT[:, :], work[:, 1, :], ACT.Copy).then_inc(xfT_ready, 1)
                        for k in new_units(s):
                            relu(b, k)
                        if s == 11:
                            act.wait_ge(route, RT * b + 3)
                            act.activation(ex[:, :, :], ex[:, :, :], ACT.Exp).then_inc(route_exp, 1)
                        if s == 12:
                            act.wait_ge(pc_filled, NPC * b + 4)
                            act.activation(wrT[:, :], work[0:E, 0, :], ACT.Copy).then_inc(wrT_ready, 1)
                    if ahead:
                        b = it + 1
                        if s == 4:
                            if isinstance(it, int) and it < 0:
                                act.wait_ge(pads_made, 1)
                            act.wait_ge(norm_a, 4 * b + 2)
                            inverse_deviation(rs, mv[:, :, 1], rs_ready, 4 * b + 2)
                        if s == 5:
                            act.wait_ge(norm_a, 4 * b + 4)
                            inverse_deviation(rs2, rq[:, 1, :], rs_ready, 4 * b + 4)
                        if s == 6:
                            act.wait_ge(rs_ready, 4 * b + 4)
                            act.wait_ge(xh_ready, b + 1)
                            for i in range(NT):
                                last = act.activation(xn[:, i, :], xha[:, i, :], ACT.Copy, scale=rs2[:, i:i + 1])
                            last.then_inc(xn_ready, 1)
                        if s == 8:
                            read_proj(b, 0, xnT[:, TAPS - 1:], work[:, 1, :], ACT.Identity,
                                      scale=cols[:, GC:GC + 1], bias=cols[:, BC:BC + 1])
                        if s in (12, 13):
                            if s == 12:
                                reach(act, (uz_copied, 16 * (it + 1)))
                            read_proj(b, s - 11, uza[:, NH + s - 12, :], work[:, 1, :], ACT.Copy)
                        if s in (14, 15):
                            read_proj(b, s - 11, uza[:, s - 14, :], work[:, 15 - s, :], ACT.Identity,
                                      bias=cols[:, CBC + s - 14:CBC + s - 13])
                        if s == 16:
                            act.wait_ge(pa_read, NPA * b + 5)
                            act.activation(uza[:, :, :], uza[:, :, :], ACT.Silu).then_inc(silu_done, 1)
                            act.preload_act_table_set(EXP_LN_TABLES)
                        if s == 18:
                            reach(act, (xd_stored, 16 * (it + 1)))
                            read_proj(b, 5, xd[:, :], work[0:NX, 1, :], ACT.Copy)
                        for h, s0 in ((0, 19), (1, 22)):
                            c = 6 * (NH * b + h)
                            if s == s0:
                                pairs = NP // NH * (h + 1)
                                for r in range(RING):
                                    n = 32 * ((NP // RING) * it + pairs // RING)
                                    reach(act, (du_spread[r], n), (delta_spread[r], n))
                                bias = cols[:, DTC + h:DTC + h + 1]
                                act.wait_ge(pa_filled, NPA * b + 7 + h)
                                act.activation(delta[:, h, :], work[:, h, :], ACT.Abs, bias=bias)
                                read_proj(b, 6 + h, du[:, h, :], work[:, h, :], ACT.Relu, bias=bias)
                                act.wait_ge(pa_read, NPA * b + 7 + h)
                                act.activation(delta[:, h, :], delta[:, h, :], ACT.Exp, scale=-1.0).then_inc(soft, 1)
                                act.wait_ge(soft, c + 1)
                                act.activation(sp1[:, h, :], delta[:, h, :], ACT.Ln, bias=csts[:, 1:2]).then_inc(soft, 1)
                                act.wait_ge(soft, c + 2)
                                act.activation(sp1[:, h, :], sp1[:, h, :], ACT.Exp, scale=-1.0).then_inc(soft, 1)
                            if s == s0 + 2:
                                act.wait_ge(lp_ready, 3 * (NH * b + h) + 1)
                                act.activation(delta[:, h, :], sp1[:, h, :], ACT.Square).then_inc(soft, 1)
                                act.wait_ge(soft, c + 4)
                                act.activation(sp2[:, h, :], delta[:, h, :], ACT.Square, bias=csts[:, 2:3]).then_inc(soft, 1)
                                act.wait_ge(soft, c + 5)
                                act.activation(sp2[:, h, :], sp2[:, h, :], ACT.Square, bias=csts[:, 3:4],
                                               scale=L1P_K).then_inc(soft, 1)

            over_batches(act, iteration)

        @block.tensor
        def _(pe):
            pe.wait_ge(rows_loaded, 7 * 16)
            pe.wait_ge(const_made, 6)
            pe.transpose(work[:, 0, 0:NROW], rows[0:NROW, :], ident[0:NROW, 0:NROW]).then_inc(cols_turned, 1)

            def sum_states(it, j):
                pe.wait_ge(hc_done, NP * it + j + 1)
                if 2 * j % (NG // NH) == 0:
                    h = 2 * j // (NG // NH)
                    reach(pe, (y_skip, NH * (it - 1) + h + 1))
                for i in range(2):
                    g = 2 * j + i
                    strip = 32 * ((g // GQ) % (P // 32))
                    last = pe.matmul(ypsum[strip:strip + 32, g * CG // P, :], sel[:, g % GQ, :],
                                     uring[:, j % RING, i, :], start=(g % GQ == 0), stop=(g % GQ == GQ - 1),
                                     tile_position=(0, strip))
                last.then_inc(summed, 1)

            def proj(b, k, products):
                for n, (o, w, r) in enumerate(products):
                    last = pe.matmul(o, w, r, start=(n == 0), stop=(n == len(products) - 1))
                last.then_inc(pa_filled, 1)

            def ffn(b, k):
                if k < UN:
                    e, f = k // FC, k % FC
                    if k == 0:
                        pe.wait_ge(xfT_ready, b + 1)
                    reach(pe, (relu_done, UN * b + k - 1))
                    pe.matmul(hpsum[:, k % 2, :], w1[:, e, f * P:(f + 1) * P], xfT[:, :],
                              start=True, stop=True).then_inc(h_filled, 1)
                if k >= LAG:
                    e, i = (k - LAG) // FC, (k - LAG) % FC
                    pe.wait_ge(relu_done, UN * b + FC * (e + 1))
                    if i == 0:
                        reach(pe, (acc_done, E * b + e - 1))
                    for f in range(FC):
                        last = pe.matmul(opsum[:, e % 2, i * P:(i + 1) * P], hb[:, e % 2, f, i * P:(i + 1) * P],
                                         w2[:, e, f, :], start=(f == 0), stop=(f == FC - 1))
                    last.then_inc(o_filled, 1)

            def iteration(it, ahead, scan, post, late):
                for s in range(SS):
                    if post and s in (0, 2):
                        sum_states(it - 1, NP - 2 + s // 2)
                    if scan and s >= 4 and s % 2 == 0:
                        sum_states(it, s // 2 - 2)
                    if late:
                        for k in old_units(s):
                            ffn(it - 2, k)
                    if ahead and s == 7:
                        pe.wait_ge(xn_ready, it + 2)
                        reach(pe, (pa_read, NPA * (it + 1)))
                        for i in range(NT):
                            last = pe.transpose(work[:, 1, i * P:(i + 1) * P], xn[:, i, :], ident[:, :])
                        last.then_inc(pa_filled, 1)
                    if post:
                        b = it - 1
                        if s == 5:
                            if isinstance(it, int) and it == 1:
                                pe.wait_ge(ffn_loaded, 16 * (4 + 2 * E))
                            pe.wait_ge(gated, NH * (b + 1))
                            pe.wait_ge(pa_read, NPA * (it + 1) if scan else NPA * NBATCH)
                            for i in range(NT):
                                for h in range(NH):
                                    last = pe.matmul(work[:, 0, i * P:(i + 1) * P], yg[:, h, i * P:(i + 1) * P],
                                                     wout[:, h, :], start=(h == 0), stop=(h == NH - 1))
                            last.then_inc(pc_filled, 1)
                        if s == 9:
                            reach(pe, (pa_read, NPA * (it + 1) + 1 if ahead else 0))
                            pe.wait_ge(xf_ready, b + 1)
                            for i in range(NT):
                                last = pe.transpose(work[:, 1, i * P:(i + 1) * P], r1[:, i, :], ident[:, :])
                            last.then_inc(pc_filled, 1)
                        if s == 10:
                            pe.wait_ge(xfT_ready, b + 1)
                            pe.wait_ge(r1_ready, b + 1)
                            for i in range(NT):
                                last = pe.matmul(work[:, 0, i * E:(i + 1) * E], xfT[:, i * P:(i + 1) * P],
                                                 wrt[:, :], start=True, stop=True)
                            last.then_inc(pc_filled, 1)
                        for k in new_units(s):
                            ffn(b, k)
                        if s == 12:
                            pe.wait_ge(w_ready, b + 1)
                            for i in range(NT):
                                last = pe.transpose(work[0:E, 0, i * P:(i + 1) * P], wr[:, i, :], ident[:, :])
                            last.then_inc(pc_filled, 1)
                        if s == 13:
                            pe.wait_ge(wrT_ready, b + 1)
                            for i in range(NT):
                                last = pe.matmul(work[:, 0, i * P:(i + 1) * P], wrT[:, i * P:(i + 1) * P],
                                                 b2s[:, :], start=True, stop=True)
                            last.then_inc(pc_filled, 1)
                    if ahead:
                        b = it + 1
                        if s == 11:
                            reach(pe, (xfT_ready, it))
                            pe.wait_ge(pa_read, NPA * b + 1)
                            if isinstance(it, int) and it < 0:
                                pe.wait_ge(w_folded, 1)
                                pe.wait_ge(cols_copied, 1)
                        if s in (11, 12):
                            h = s - 11
                            if h == 1:
                                pe.wait_ge(pa_read, NPA * b + 2)
                            proj(b, 1 + h, [(work[:, 1, :], win[:, DI + h * P:DI + (h + 1) * P], xnT[:, TAPS - 1:])])
                        if s in (13, 14):
                            h = s - 13
                            pe.wait_ge(pa_read, NPA * b + 3)
                            if h == 1:
                                reach(pe, (b2_added, it))
                            proj(b, 3 + h, [(work[:, 1 - h, :], wconv[:, k, h * P:(h + 1) * P], xnT[:, k:k + T])
                                            for k in range(TAPS)])
                        if s == 17:
                            pe.wait_ge(silu_done, b + 1)
                            for c0 in range(0, NX, 32):
                                c1 = min(c0 + 32, NX)
                                for h in range(NH):
                                    last = pe.matmul(work[c0:c1, 1, :], wxp[:, h, c0:c1], uza[:, h, :], start=(h == 0),
                                                     stop=(h == NH - 1), tile_position=(0, c0))
                            last.then_inc(pa_filled, 1)
                        if s == 18:
                            pe.wait_ge(pa_read, NPA * b + 6)
                            for h in range(NH):
                                proj(b, 6 + h, [(work[:, h, :], wdt[:, h * P:(h + 1) * P], xd[0:RANK, :])])

            over_batches(pe, iteration)

        @block.vector
        def _(dve):
            for k, c in enumerate((EPS, 2.0, L1P_A, L1P_KB)):
                dve.memset(csts[:, k:k + 1], c)
            dve.memset(xnT[:, 0:TAPS - 1], 0.0).then_inc(pads_made, 1)
            dve.wait_ge(const_made, 3)
            dve.tensor_copy(iota_f[:, :], iota_i[:, :]).then_inc(pads_made, 1)
            dve.wait_ge(proj_loaded, 4 * 16)
            for k in range(TAPS):
                last = dve.tensor_tensor(wconv[:, k, :], win[:, 0:DI], cwb[:, :].rearrange("p (c k) -> p k c", k=TAPS)[:, k, :],
                                  ALU.mult)
            last.then_inc(w_folded, 1)
            dve.wait_ge(a_exp, 1)
            dve.tensor_scalar(Amat[:, :], Amat[:, :], -1.0, None, ALU.mult).then_inc(a_made, 1)

            def token_stats(src, st_, mv_, steps, base):
                for i in range(NT):
                    last = dve.bn_stats(st_[:, i, :], src[:, i, :])
                last.then_inc(steps, 1)
                dve.wait_ge(steps, base + 1)
                dve.memset(fence[:, :], 0.0)
                for i in range(NT):
                    last = dve.bn_aggr(mv_[:, i, :], st_[:, i, :])
                last.then_inc(steps, 1)

            def normalize(dst, src, mv_, rs_):
                for i in range(NT):
                    last = dve.tensor_scalar(dst[:, i, :], src[:, i, :], mv_[:, i, 0:1], rs_[:, i:i + 1],
                                             ALU.subtract, ALU.mult)
                return last

            def stats_ahead(b):
                dve.wait_ge(x_loaded, 16 * (b + 1))
                token_stats(xa, st, mv, norm_a, 4 * b)

            def layernorms_ahead(b):
                dve.wait_ge(rs_ready, 4 * b + 2)
                reach(dve, (xh_stored, 16 * b))
                reach(dve, (xn_ready, b))
                normalize(xha, xa, mv, rs).then_inc(xh_ready, 1)
                dve.tensor_tensor(rq[:, 0, :], mv[:, :, 1], rs[:, :], ALU.mult).then_inc(norm_a, 1)
                dve.wait_ge(norm_a, 4 * b + 3)
                dve.tensor_tensor(rq[:, 1, :], rq[:, 0, :], rs[:, :], ALU.mult).then_inc(norm_a, 1)

            def log1p_argument(b, h):
                dve.wait_ge(soft, 6 * (NH * b + h) + 3)
                dve.tensor_tensor(sp1[:, h, :], sp1[:, h, :], delta[:, h, :], ALU.mult).then_inc(lp_ready, 1)

            def step_size(b, h):
                c = 3 * (NH * b + h)
                dve.wait_ge(soft, 6 * (NH * b + h) + 6)
                dve.scalar_tensor_tensor(out=sp2[:, h, :], in0=delta[:, h, :], scalar=L1P_D, in1=sp2[:, h, :],
                                         op0=ALU.mult, op1=ALU.add).then_inc(lp_ready, 1)
                dve.wait_ge(lp_ready, c + 2)
                dve.scalar_tensor_tensor(out=sp2[:, h, :], in0=sp2[:, h, :], scalar=L1P_E, in1=sp1[:, h, :],
                                         op0=ALU.add, op1=ALU.mult).then_inc(lp_ready, 1)
                dve.wait_ge(lp_ready, c + 3)
                dve.scalar_tensor_tensor(out=delta[:, h, :], in0=sp2[:, h, :], scalar=2.0, in1=du[:, h, :],
                                         op0=ALU.mult, op1=ALU.add).then_inc(delta_ready, 1)

            def drive(it, j):
                if j == 0:
                    dve.wait_ge(b_loaded, 16 * (it + 1))
                dve.wait_ge(du_spread[j % RING], 32 * ((NP // RING) * it + j // RING + 1))
                v = uring[:, j % RING, :, :]
                bb = bcc[:, 0, :].unsqueeze(1).broadcast_to([P, 2, T])
                dve.tensor_tensor(v, v, bb, ALU.mult).then_inc(db_done, 1)

            def scan_group(it, g):
                j, i = g // 2, g % 2
                if i == 0:
                    dve.wait_ge(db_done, NP * it + j + 1)
                dve.wait_ge(exp_done, NG * it + g + 1)
                v = uring[:, j % RING, i, :]
                ins = dve.tensor_tensor_scan(v, dring[:, j % RING, i, :], v, 0.0, ALU.mult, ALU.add)
                if i == 1:
                    ins.then_inc(scan_done, 1)

            def skip(b, h):
                if h == 0:
                    dve.wait_ge(uz_copied, 16 * (b + 1))
                    reach(dve, (pc_filled, NPC * (b - 1) + 1))
                dve.wait_ge(summed, NP * b + NP // NH * (h + 1))
                dve.scalar_tensor_tensor(out=yg[:, h, :], in0=uzc[:, h, :], scalar=cols[:, DSC + h:DSC + h + 1],
                                         in1=ypsum[:, h, :], op0=ALU.mult, op1=ALU.add).then_inc(y_skip, 1)

            def residual(b):
                dve.wait_ge(pc_filled, NPC * b + 1)
                dve.wait_ge(xc_loaded, 32 * (b + 1))
                dve.tensor_tensor(r1[:, :, :], work[:, 0, :].rearrange("p (i d) -> p i d", d=D), xhc[:, :, :],
                                  ALU.add).then_inc(r1_ready, 1)
                dve.wait_ge(r1_ready, b + 1)
                token_stats(r1, stc, mvc, norm_c, 5 * b)

            def residual_normed(b):
                dve.wait_ge(rsc_ready, 4 * b + 2)
                normalize(r1, r1, mvc, rsc).then_inc(norm_c, 1)
                dve.wait_ge(norm_c, 5 * b + 3)
                reach(dve, (x1_copied, 16 * b))
                dve.tensor_tensor(x1[:, :, :], r1[:, :, :], xc[:, :, :], ALU.add).then_inc(x1_ready, 1)
                dve.wait_ge(x1_ready, b + 1)
                token_stats(x1, stc, mvc, norm_c, 5 * b + 3)

            def experts_input(b):
                dve.wait_ge(rsc_ready, 4 * b + 4)
                normalize(r1, x1, mvc, rsc).then_inc(xf_ready, 1)

            def top_two(b):
                dve.wait_ge(pc_filled, NPC * b + 3)
                dve.tensor_tensor(lg[:, :, :], work[:, 0, 0:NT * E].rearrange("p (i e) -> p i e", e=E),
                                  brb[:, :].unsqueeze(1).broadcast_to([P, NT, E]), ALU.add).then_inc(route, 1)
                dve.wait_ge(route, RT * b + 1)
                dve.memset(fence[:, :], 0.0)
                for i in range(NT):
                    last = dve.max(mx[:, i, :], lg[:, i, :])
                last.then_inc(route, 1)
                dve.wait_ge(route, RT * b + 2)
                dve.tensor_tensor(ex[:, :, :], lg[:, :, :], mx[:, :, 0:1].broadcast_to([P, NT, E]),
                                  ALU.subtract).then_inc(route, 1)
                for i in range(NT):
                    last = dve.max_index(ix[:, i, :], mx[:, i, :], lg[:, i, :])
                last.then_inc(route, 1)
                dve.wait_ge(route, RT * b + 4)
                dve.tensor_copy(ixf[:, :, :], ix[:, :, 0:2]).then_inc(route, 1)
                dve.wait_ge(route, RT * b + 5)
                numbers = iota_f[:, :].unsqueeze(1).broadcast_to([P, NT, E])
                dve.tensor_tensor(m1[:, :, :], numbers, ixf[:, :, 0:1].broadcast_to([P, NT, E]), ALU.is_equal)
                dve.tensor_tensor(m2[:, :, :], numbers, ixf[:, :, 1:2].broadcast_to([P, NT, E]), ALU.is_equal
                                  ).then_inc(route, 1)
                dve.wait_ge(route, RT * b + 6)
                dve.tensor_tensor(m1[:, :, :], m1[:, :, :], m2[:, :, :], ALU.add).then_inc(route, 1)

            def softmax(b):
                dve.wait_ge(route_exp, b + 1)
                dve.wait_ge(route, RT * b + 7)
                dve.tensor_tensor(ex[:, :, :], ex[:, :, :], m1[:, :, :], ALU.mult).then_inc(route, 1)
                dve.wait_ge(route, RT * b + 8)
                dve.tensor_reduce(sm[:, :], ex[:, :, :], AX.X, ALU.add).then_inc(route, 1)
                dve.wait_ge(route, RT * b + 9)
                dve.reciprocal(sm[:, :], sm[:, :]).then_inc(route, 1)
                dve.wait_ge(route, RT * b + 10)
                dve.tensor_tensor(wr[:, :, :], ex[:, :, :], sm[:, :].unsqueeze(2).broadcast_to([P, NT, E]),
                                  ALU.mult).then_inc(w_ready, 1)

            def start_sum(b):
                dve.wait_ge(pc_filled, NPC * b + 5)
                dve.tensor_copy(acc[:, :, :], work[:, 0, :].rearrange("p (i d) -> p i d", d=D)).then_inc(b2_added, 1)

            def add_expert(b, e):
                dve.wait_ge(o_filled, UN * b + FC * (e + 1))
                if e == 0:
                    dve.wait_ge(b2_added, b + 1)
                else:
                    dve.wait_ge(acc_done, E * b + e)
                for i in range(NT):
                    last = dve.scalar_tensor_tensor(out=acc[:, i, :], in0=opsum[:, e % 2, i * P:(i + 1) * P],
                                                    scalar=wr[:, i, e:e + 1], in1=acc[:, i, :],
                                                    op0=ALU.mult, op1=ALU.add)
                last.then_inc(acc_done, 1)

            def output(b):
                dve.wait_ge(acc_done, E * (b + 1))
                token_stats(acc, sto, mvo, norm_o, 3 * b)

            def output_normed(b):
                dve.wait_ge(rso_ready, 2 * b + 2)
                dve.wait_ge(x1_copied, 16 * (b + 1))
                normalize(xo, acc, mvo, rso).then_inc(norm_o, 1)
                dve.wait_ge(norm_o, 3 * b + 3)
                dve.tensor_tensor(xo[:, :, :], xo[:, :, :], x1e[:, :, :], ALU.add).then_inc(out_ready, 1)

            def iteration(it, ahead, scan, post, late):
                for s in range(SS):
                    if scan and s % 2 == 0:
                        drive(it, s // 2)
                    if scan:
                        scan_group(it, s)
                    if late:
                        if s in (1, 3, 5, 7):
                            add_expert(it - 2, E - FC + s // 2)
                        if s == 8:
                            output(it - 2)
                        if s == 9:
                            output_normed(it - 2)
                    if post:
                        if s == 3:
                            skip(it - 1, 1)
                        if s == 6:
                            residual(it - 1)
                        if s == 7:
                            residual_normed(it - 1)
                        if s == 8:
                            experts_input(it - 1)
                        if s == 10:
                            if isinstance(it, int) and it == 1:
                                dve.wait_ge(pads_made, 2)
                                dve.wait_ge(ffn_loaded, 16 * (4 + 2 * E))
                            top_two(it - 1)
                        if s == 11:
                            softmax(it - 1)
                        if s == 13:
                            start_sum(it - 1)
                        if s in (17, 21, 25, 29):
                            add_expert(it - 1, (s - 17) // 4)
                    if ahead and s in (20, 23):
                        log1p_argument(it + 1, (s - 20) // 3)
                    if ahead and s in (22, 25):
                        step_size(it + 1, (s - 22) // 3)
                    if ahead and s == 4:
                        stats_ahead(it + 1)
                    if ahead and s == 5:
                        layernorms_ahead(it + 1)
                    if scan and s == 19:
                        skip(it, 0)

            over_batches(dve, iteration)


_INS = ['x', 'ln_g', 'ln_b', 'W_in', 'conv_w', 'conv_b', 'W_xp', 'W_dt', 'dt_bias', 'A_log', 'D_skip', 'W_out']
_FFN = ['W_router', 'b_router', 'W1', 'b1', 'W2', 'b2']


def kernel(**inputs):
    import numpy as _np
    import concourse.bacc as _bacc
    from concourse import mybir as _mybir
    from concourse.bass_utils import run_bass_kernel_spmd as _run

    nc = _bacc.Bacc("TRN2", target_bir_lowering=False, num_devices=1)
    arrays, args = {}, []
    for name in [f"L0_attn_{n}" for n in _INS] + [f"L0_ffn_{n}" for n in _FFN]:
        a = _np.ascontiguousarray(inputs[name])
        arrays[f"in_{name}"] = a
        args.append(nc.dram_tensor(f"in_{name}", a.shape, _mybir.dt.from_np(a.dtype), kind="ExternalInput").ap())
    shape = inputs["L0_attn_x"].shape
    args.append(nc.dram_tensor("out_x", shape, _mybir.dt.float32, kind="ExternalOutput").ap())
    mamba_moe_kernel(nc, *args)
    r = _run(nc, [arrays], core_ids=[0])
    return r.results[0]["out_x"]
```

```python
from contextlib import ExitStack

import concourse.bass as bass
from concourse import mybir

F32 = mybir.dt.float32
F32R = mybir.dt.float32r
U32 = mybir.dt.uint32
I32 = mybir.dt.int32
ALU = mybir.AluOpType
ACT = mybir.ActivationFunctionType
AX = mybir.AxisListType

P = 128
EPS = 1e-5
L1P_A, L1P_K, L1P_KB = 0.24810788804420705, 0.3753309023989405, 0.19728378793895784
L1P_D, L1P_E = 0.25123911755073414, 0.9514290285127261
EXP_LN_TABLES = "natural_log_exp_and_others"


def reach(eng, *waits):
    waits = [(sem, count) for sem, count in waits if not (isinstance(count, int) and count <= 0)]
    for _, count in waits:
        if not isinstance(count, int):
            eng.compute_val(count)
    for sem, count in waits:
        eng.wait_ge(sem, count)


def mamba_moe_kernel(nc, x, ln_g, ln_b, W_in, conv_w, conv_b, W_xp, W_dt, dt_bias, A_log, D_skip,
                     W_out, W_router, b_router, W1, b1, W2, b2, out):
    NBATCH, T, D = x.shape
    DI = D_skip.shape[0]
    NST = A_log.shape[1]
    TAPS = conv_w.shape[2]
    RANK = W_dt.shape[0]
    E, _, DF = W1.shape
    assert D == P and T == 512 and DI == 2 * P and E == 8 and P % NST == 0
    NT = T // P
    NH = DI // P
    CG = P // NST
    NG = DI // CG
    NP = NG // 2
    GQ = 32 // CG
    FC = DF // P
    UN = E * FC
    LAG = 5
    RING, PRE = 8, 4
    SS = NG
    NEW0 = 10
    SPLIT = 24
    LEAD = 4
    RT = 10
    NPA, NPC = 8, 5

    ctx = ExitStack()
    with ctx:
        def sb(name, shape, dt=F32):
            return ctx.enter_context(nc.sbuf_tensor(name, shape, dt))

        def ps(name, shape):
            return ctx.enter_context(nc.psum_tensor(name, shape, F32))

        def sem(name):
            return ctx.enter_context(nc.semaphore(name))

        NROW = NG + UN + 3 * NH + 2
        rows = sb("rows", [P, P])
        cols = sb("cols", [P, NROW])
        Amat = sb("Amat", [P, NG])
        wz = sb("wz", [P, DI])
        wconv = sb("wconv", [P, TAPS, DI])
        wxp = sb("wxp", [P, NH, RANK + 2 * NST])
        wdt = sb("wdt", [RANK, DI])
        wout = sb("wout", [P, NH, D])
        wrt = sb("wrt", [P, E])
        wrh, wrl = sb("wrh", [P, E], F32R), sb("wrl", [P, E], F32R)
        w1h, w1l = sb("w1h", [P, E, DF], F32R), sb("w1l", [P, E, DF], F32R)
        xfh, xfl = sb("xfh", [P, T], F32R), sb("xfl", [P, T], F32R)
        brb = sb("brb", [P, E])
        w2 = sb("w2", [P, E, FC, D])
        b2s = sb("b2s", [E, D])
        ident = sb("ident", [P, P])
        sel = sb("sel", [P, GQ, 32])
        iota_i = sb("iota_i", [P, E], I32)
        iota_f = sb("iota_f", [P, E])
        B1C = NG
        CBC, DTC, DSC, GC, BC = (B1C + UN + k for k in (0, NH, 2 * NH, 3 * NH, 3 * NH + 1))

        xa = sb("xa", [P, NT, D])
        xha = sb("xha", [P, NT, D])
        xnT = sb("xnT", [P, TAPS - 1 + T])
        uza = sb("uza", [P, 2 * NH, T])
        NX = RANK + 2 * NST
        xd = sb("xd", [NX, T])
        delta = sb("delta", [P, NH, T])
        du = sb("du", [P, NH, T])
        st = sb("st", [P, NT, 6])
        mv = sb("mv", [P, NT, 2])
        rs = sb("rs", [P, NT])
        rq = sb("rq", [P, 2, NT])
        rs2 = sb("rs2", [P, NT])
        bcc = sb("bcc", [P, 2, T])
        dring = sb("dring", [P, RING, 2, T])
        uring = sb("uring", [P, RING, 2, T])
        assert E * DF == (RING - PRE) * 2 * T and TAPS * DI <= 2 * T and DI <= T
        w1_raw = dring[:, PRE:, :, :].rearrange("p r i t -> p (r i t)").rearrange("p (e n) -> p e n", e=E)
        conv_raw = uring[:, PRE, :, :].rearrange("p i t -> p (i t)")[:, 0:TAPS * DI]
        win_raw = uring[:, PRE + 1, 0, 0:DI]
        uzc = sb("uzc", [P, 2 * NH, T])
        xc = sb("xc", [P, NT, D])
        xhc = sb("xhc", [P, NT, D])
        yg = sb("yg", [P, NH, T])
        r1 = sb("r1", [P, NT, D])
        x1 = sb("x1", [P, NT, D])
        stc = sb("stc", [P, NT, 6])
        mvc = sb("mvc", [P, NT, 2])
        rsc = sb("rsc", [P, NT])
        sto = sb("sto", [P, NT, 6])
        mvo = sb("mvo", [P, NT, 2])
        rso = sb("rso", [P, NT])
        fence = sb("fence", [P, 1])
        csts = sb("csts", [P, 4])
        sp1 = sb("sp1", [P, NH, T])
        sp2 = sb("sp2", [P, NH, T])
        lg = sb("lg", [P, NT, E])
        mx = sb("mx", [P, NT, E])
        ix = sb("ix", [P, NT, E], U32)
        ixf = sb("ixf", [P, NT, 2])
        m1 = sb("m1", [P, NT, E])
        m2 = sb("m2", [P, NT, E])
        ex = sb("ex", [P, NT, E])
        sm = sb("sm", [P, NT])
        wr = sb("wr", [P, NT, E])
        wrT = sb("wrT", [E, T])
        hb = sb("hb", [P, 2, FC, T])
        acc = sb("acc", [P, NT, D])
        x1e = sb("x1e", [P, NT, D])
        xo = sb("xo", [P, NT, D])
        xn = xo

        xd_dram = nc.dram_tensor("xd_dram", [NBATCH, NX, T], F32, kind="Internal").ap()
        xh_dram = nc.dram_tensor("xh_dram", [NBATCH, P, NT * D], F32, kind="Internal").ap()

        ypsum = ps("ypsum", [P, NH, T])
        hpsum = ps("hpsum", [P, 2, T])
        opsum = ps("opsum", [P, 2, T])
        work = ps("work", [P, 2, T])

        rows_loaded, proj_loaded, ffn_loaded = sem("rows_loaded"), sem("proj_loaded"), sem("ffn_loaded")
        w1_loaded, high_made, low_made = sem("w1_loaded"), sem("high_made"), sem("low_made")
        const_made, cols_turned, cols_copied, a_exp = (sem("const_made"), sem("cols_turned"),
                                                       sem("cols_copied"), sem("a_exp"))
        a_made, w_folded, pads_made = sem("a_made"), sem("w_folded"), sem("pads_made")
        x_loaded, xc_loaded, uz_copied = sem("x_loaded"), sem("xc_loaded"), sem("uz_copied")
        b_loaded, c_loaded, x1_copied = sem("b_loaded"), sem("c_loaded"), sem("x1_copied")
        xd_stored, xh_stored = sem("xd_stored"), sem("xh_stored")
        out_stored = sem("out_stored")
        delta_spread = [sem(f"delta_spread{r}") for r in range(RING)]
        du_spread = [sem(f"du_spread{r}") for r in range(RING)]
        norm_a, xh_ready = sem("norm_a"), sem("xh_ready")
        db_done, scan_done, y_skip = sem("db_done"), sem("scan_done"), sem("y_skip")
        norm_c, r1_ready, x1_ready, xf_ready = (sem("norm_c"), sem("r1_ready"), sem("x1_ready"),
                                                sem("xf_ready"))
        route, w_ready, b2_added = sem("route"), sem("w_ready"), sem("b2_added")
        acc_done, norm_o, out_ready = sem("acc_done"), sem("norm_o"), sem("out_ready")
        rs_ready, rsc_ready, rso_ready = sem("rs_ready"), sem("rsc_ready"), sem("rso_ready")
        xn_ready, pa_read, silu_done = sem("xn_ready"), sem("pa_read"), sem("silu_done")
        lp_ready = sem("lp_ready")
        soft, exp_done = [sem(f"soft{h}") for h in range(NH)], sem("exp_done")
        xfh_ready, xfl_ready, route_exp, wrT_ready = sem("xfh_ready"), sem("xfl_ready"), sem("route_exp"), sem("wrT_ready")
        relu_done = sem("relu_done")
        hc_done, delta_ready, du_ready, gated = (sem("hc_done"), sem("delta_ready"), sem("du_ready"),
                                                 sem("gated"))
        summed, pa_filled, pc_filled = sem("summed"), sem("pa_filled"), sem("pc_filled")
        h_filled, o_filled = sem("h_filled"), sem("o_filled")

        def over_batches(eng, iteration):
            def flags(it):
                return dict(ahead=it + 1 < NBATCH, scan=0 <= it < NBATCH, post=0 <= it - 1 < NBATCH,
                            late=0 <= it - 2 < NBATCH)
            for it in (-1, 0, 1):
                iteration(it, **flags(it))
            with eng.Fori(2, NBATCH - 1) as it:
                iteration(it, ahead=True, scan=True, post=True, late=True)
            for it in (NBATCH - 1, NBATCH, NBATCH + 1):
                iteration(it, **flags(it))

        def new_units(s):
            n = s - NEW0
            return [2 * n, 2 * n + 1] if 0 <= n < 2 else [n + 2] if n >= 2 else []

        def old_units(s):
            cut = [24, 26, 27, 28, 30, 31, 32, 34, 35, 35, 36, 37]
            return list(range(cut[s], cut[s + 1])) if s + 1 < len(cut) else []
        assert SS - NEW0 + 2 == SPLIT and UN + LAG == 37

        block = ctx.enter_context(nc.Block())

        @block.sync
        def _(sp):
            sp.dma_start(rows[0:NG, :], A_log.rearrange("(g c) n -> g (c n)", c=CG)).then_inc(rows_loaded, 16)
            sp.dma_start(rows[B1C:B1C + UN, :], b1.rearrange("e (f p) -> (e f) p", p=P)).then_inc(rows_loaded, 16)
            for at, v in ((CBC, conv_b), (DTC, dt_bias), (DSC, D_skip), (GC, ln_g), (BC, ln_b)):
                k = v.shape[0] // P
                sp.dma_start(rows[at:at + k, :], v.rearrange("(h p) -> h p", p=P)).then_inc(rows_loaded, 16)
            sp.dma_start(xa[:, :, :], x[0].rearrange("(i p) d -> p i d", p=P)).then_inc(x_loaded, 16)
            sp.dma_start(win_raw, W_in[:, 0:DI]).then_inc(proj_loaded, 16)
            sp.dma_start(wz[:, :], W_in[:, DI:2 * DI]).then_inc(proj_loaded, 16)
            sp.dma_start(conv_raw, conv_w.rearrange("c a k -> (c a k)").partition_broadcast(P)).then_inc(proj_loaded, 16)
            sp.dma_start(wxp[:, :, :], W_xp.rearrange("(h p) n -> p h n", p=P)).then_inc(proj_loaded, 16)
            sp.dma_start(wdt[:, :], W_dt).then_inc(proj_loaded, 16)
            sp.dma_start(w1_raw, W1.rearrange("e d n -> d e n")).then_inc(w1_loaded, 16)
            sp.dma_start(wrt[:, :], W_router).then_inc(w1_loaded, 16)
            sp.dma_start(wout[:, :, :], W_out.rearrange("(h p) n -> p h n", p=P)).then_inc(ffn_loaded, 16)
            sp.dma_start(brb[:, :], b_router.partition_broadcast(P)).then_inc(ffn_loaded, 16)
            sp.dma_start(b2s[:, :], b2).then_inc(ffn_loaded, 16)
            for e in range(E):
                sp.dma_start(w2[:, e, :, :], W2[e].rearrange("(f p) n -> p f n", p=P)).then_inc(ffn_loaded, 16)

            def spread(it, j):
                pair = NP * it + j
                made = [(du_ready, NH * it + j // (NP // NH) + 1)] if j % (NP // NH) == 0 else []
                reach(sp, *made, (summed, pair - RING + 1))
                for i in range(2):
                    g = 2 * j + i
                    c0 = (g * CG) % P
                    for src, ring, n, loaded in ((delta, dring, RING, delta_spread), (du, uring, RING, du_spread)):
                        rowsrc = src[c0:c0 + CG, g * CG // P, :].unsqueeze(1).broadcast_to([CG, NST, T])
                        sp.dma_start(ring[:, j % n, i, :], rowsrc).then_inc(loaded[j % n], 16)

            def iteration(it, ahead, scan, post, late):
                if ahead and not (isinstance(it, int) and it < 0):
                    sp.wait_ge(xh_ready, it + 1)
                    sp.dma_start(xa[:, :, :], x[bass.ds(it + 1, 1)].rearrange("a (i p) d -> p (a i) d", p=P)
                                 ).then_inc(x_loaded, 16)
                if scan:
                    for k, (used, loaded) in enumerate(((db_done, b_loaded), (hc_done, c_loaded))):
                        reach(sp, *([] if k else [(xd_stored, 16 * (it + 1))]), (used, NP * it))
                        n0 = RANK + k * NST
                        sp.dma_start(bcc[:, k, :], xd_dram[bass.ds(it, 1), n0:n0 + NST, :].broadcast_to([CG, NST, T])
                                     ).then_inc(loaded, 16)
                    if isinstance(it, int) and it == 0:
                        sp.wait_ge(low_made, 2)
                        sp.wait_ge(w_folded, 1)
                    spread(it, 4)
                    spread(it, 5)
                    reach(sp, (gated, NH * it))
                    sp.dma_start(uzc[:, :, :], uza[:, :, :]).then_inc(uz_copied, 16)
                if ahead:
                    sp.wait_ge(xh_ready, it + 2)
                    sp.dma_start(xh_dram[bass.ds(it + 1, 1)].rearrange("a p n -> p (a n)"),
                                 xha[:, :, :].rearrange("p i d -> p (i d)")).then_inc(xh_stored, 16)
                if scan:
                    spread(it, 6)
                    spread(it, 7)
                    reach(sp, (x1_ready, it))
                    sp.wait_ge(xh_stored, 16 * (it + 1))
                    sp.dma_start(xc[:, :, :], x[bass.ds(it, 1)].rearrange("a (i p) d -> p (a i) d", p=P)
                                 ).then_inc(xc_loaded, 16)
                    sp.dma_start(xhc[:, :, :].rearrange("p i d -> p (i d)"),
                                 xh_dram[bass.ds(it, 1)].rearrange("a p n -> p (a n)")).then_inc(xc_loaded, 16)
                    for j in range(8, 11):
                        spread(it, j)
                if late:
                    sp.wait_ge(out_ready, it - 1)
                    sp.dma_start(out[bass.ds(it - 2, 1)].rearrange("a (i p) d -> p (a i) d", p=P), xo[:, :, :]
                                 ).then_inc(out_stored, 16)
                    sp.wait_ge(out_stored, 16 * (it - 1))
                if post:
                    sp.wait_ge(x1_ready, it)
                    sp.dma_start(x1e[:, :, :], x1[:, :, :]).then_inc(x1_copied, 16)
                if scan:
                    for j in range(11, NP):
                        spread(it, j)
                if ahead:
                    sp.wait_ge(pa_read, NPA * (it + 1) + 6)
                    sp.dma_start(xd_dram[bass.ds(it + 1, 1)].rearrange("a n t -> n (a t)"), xd[:, :]).then_inc(xd_stored, 16)
                    for j in range(PRE):
                        spread(it + 1, j)

            over_batches(sp, iteration)
            sp.wait_ge(out_stored, 16 * NBATCH)
            sp.wait_ge(xd_stored, 16 * NBATCH)
            sp.wait_ge(xh_stored, 16 * NBATCH)

        @block.gpsimd
        def _(pool):
            pool.memset(ident[:, :], 0.0).then_inc(const_made, 1)
            pool.memset(sel[:, :, :], 1.0).then_inc(const_made, 1)
            pool.iota(iota_i[:, :], [[1, E]], base=0, channel_multiplier=0).then_inc(const_made, 1)
            pool.wait_ge(const_made, 3)
            pool.affine_select(out=ident[:, :], in_=ident[:, :], compare_op=ALU.not_equal, fill=1.0, base=0,
                               pattern=[[-1, P]], channel_multiplier=1).then_inc(const_made, 1)
            pool.affine_select(out=sel[:, :, :], in_=sel[:, :, :], compare_op=ALU.is_ge, fill=0.0, base=0,
                               pattern=[[P, GQ], [-NST, 32]], channel_multiplier=1).then_inc(const_made, 1)
            pool.wait_ge(const_made, 5)
            pool.affine_select(out=sel[:, :, :], in_=sel[:, :, :], compare_op=ALU.is_ge, fill=0.0, base=NST - 1,
                               pattern=[[-P, GQ], [NST, 32]], channel_multiplier=-1).then_inc(const_made, 1)

            def states_to_output(it, j):
                if j == 0:
                    pool.wait_ge(c_loaded, 16 * (it + 1))
                pool.wait_ge(scan_done, NP * it + j + 1)
                h = uring[:, j % RING, :, :]
                c = bcc[:, 1, :].unsqueeze(1).broadcast_to([P, 2, T])
                pool.tensor_tensor(h, h, c, ALU.mult).then_inc(hc_done, 1)

            def gate(b, h):
                pool.wait_ge(y_skip, NH * b + h + 1)
                pool.tensor_tensor(yg[:, h, :], yg[:, h, :], uzc[:, NH + h, :], ALU.mult).then_inc(gated, 1)

            def steps_of_time(b, h):
                pool.wait_ge(delta_ready, NH * b + h + 1)
                pool.wait_ge(silu_done, b + 1)
                pool.tensor_tensor(du[:, h, :], delta[:, h, :], uza[:, h, :], ALU.mult).then_inc(du_ready, 1)

            def iteration(it, ahead, scan, post, late):
                for s in range(SS):
                    if s == 0 and post:
                        states_to_output(it - 1, NP - 1)
                    if s == 3 and post:
                        gate(it - 1, 1)
                    if s >= 2 and s % 2 == 0 and scan:
                        states_to_output(it, s // 2 - 1)
                    if s == 20 and scan:
                        gate(it, 0)
                    if s == 0 and isinstance(it, int) and it < 0:
                        pool.wait_ge(high_made, 2)
                        pool.tensor_tensor(wrl[:, :], wrt[:, :], wrh[:, :].bitcast(F32), ALU.subtract).then_inc(low_made, 1)
                        pool.tensor_tensor(w1l[:, :, :], w1_raw, w1h[:, :, :].bitcast(F32), ALU.subtract).then_inc(low_made, 1)
                    if s in (24, 27) and ahead:
                        steps_of_time(it + 1, (s - 24) // 3)

            over_batches(pool, iteration)

        @block.scalar
        def _(act):
            act.preload_act_table_set(EXP_LN_TABLES)
            act.wait_ge(cols_turned, 1)
            act.activation(cols[:, :], work[:, 0, 0:NROW], ACT.Copy).then_inc(cols_copied, 1)
            act.wait_ge(cols_copied, 1)
            act.activation(Amat[:, :], cols[:, 0:NG], ACT.Exp).then_inc(a_exp, 1)

            def decay(it, g):
                j, i = g // 2, g % 2
                if isinstance(it, int) and it == 0 and g == 0:
                    act.wait_ge(a_made, 1)
                if i == 0:
                    act.wait_ge(delta_spread[j % RING], 32 * ((NP // RING) * it + j // RING + 1))
                act.activation(dring[:, j % RING, i, :], dring[:, j % RING, i, :], ACT.Exp,
                               scale=Amat[:, g:g + 1]).then_inc(exp_done, 1)

            def read_proj(b, k, dst, src, func, **affine):
                act.wait_ge(pa_filled, NPA * b + k + 1)
                act.activation(dst, src, func, **affine).then_inc(pa_read, 1)

            def relu(b, u):
                e, f = u // FC, u % FC
                act.wait_ge(h_filled, UN * b + u + 1)
                if f == 0:
                    reach(act, (o_filled, UN * b + FC * (e - 1)))
                act.activation(hb[:, e % 2, f, :], hpsum[:, u % 2, :], ACT.Relu,
                               bias=cols[:, B1C + u:B1C + u + 1]).then_inc(relu_done, 1)

            def inverse_deviation(dst, var, ready, count):
                act.activation(dst[:, :], var, ACT.Ln, bias=csts[:, 0:1]).then_inc(ready, 1)
                act.wait_ge(ready, count - 1)
                act.activation(dst[:, :], dst[:, :], ACT.Exp, scale=-0.5).then_inc(ready, 1)

            def iteration(it, ahead, scan, post, late):
                for s in range(SS):
                    if scan and s + LEAD < NG:
                        decay(it, s + LEAD)
                    if ahead and s + LEAD >= NG:
                        decay(it + 1, s + LEAD - NG)
                    if ahead and s == 6:
                        read_proj(it + 1, 0, xnT[:, TAPS - 1:], work[:, 1, :], ACT.Identity,
                                  scale=cols[:, GC:GC + 1], bias=cols[:, BC:BC + 1])
                    if s == 7 and isinstance(it, int) and it < 0:
                        act.wait_ge(w1_loaded, 32)
                        act.activation(wrh[:, :], wrt[:, :], ACT.Copy).then_inc(high_made, 1)
                        act.activation(w1h[:, :, :], w1_raw, ACT.Copy).then_inc(high_made, 1)
                    if late and s == 12:
                        act.wait_ge(norm_o, 3 * (it - 2) + 2)
                        inverse_deviation(rso, mvo[:, :, 1], rso_ready, 2 * (it - 2) + 2)
                    if post:
                        b = it - 1
                        if s in (6, 7):
                            act.wait_ge(norm_c, 5 * b + (2, 5)[s - 6])
                            inverse_deviation(rsc, mvc[:, :, 1], rsc_ready, 4 * b + (2, 4)[s - 6])
                        if s == 9:
                            act.wait_ge(pc_filled, NPC * b + 2)
                            act.activation(xfh[:, :], work[:, 1, :], ACT.Copy).then_inc(xfh_ready, 1)
                        if s == 12:
                            act.wait_ge(route, RT * b + 3)
                            act.activation(ex[:, :, :], ex[:, :, :], ACT.Exp).then_inc(route_exp, 1)
                    if late:
                        for k in old_units(s):
                            if k < UN:
                                relu(it - 2, k)
                    if post:
                        for k in new_units(s):
                            relu(b, k)
                        if s == 14:
                            act.wait_ge(pc_filled, NPC * b + 4)
                            act.activation(wrT[:, :], work[0:E, 0, :], ACT.Copy).then_inc(wrT_ready, 1)
                    if ahead:
                        b = it + 1
                        if s == 2:
                            if isinstance(it, int) and it < 0:
                                act.wait_ge(pads_made, 1)
                            act.wait_ge(norm_a, 4 * b + 2)
                            inverse_deviation(rs, mv[:, :, 1], rs_ready, 4 * b + 2)
                        if s == 4:
                            act.wait_ge(norm_a, 4 * b + 4)
                            inverse_deviation(rs2, rq[:, 1, :], rs_ready, 4 * b + 4)
                        if s == 4:
                            act.wait_ge(rs_ready, 4 * b + 4)
                            act.wait_ge(xh_ready, b + 1)
                            reach(act, (x1_copied, 16 * (it - 1)))
                            for i in range(NT):
                                last = act.activation(xn[:, i, :], xha[:, i, :], ACT.Copy, scale=rs2[:, i:i + 1])
                            last.then_inc(xn_ready, 1)
                        if s in (8, 9):
                            if s == 8:
                                reach(act, (uz_copied, 16 * (it + 1)))
                            read_proj(b, s - 7, uza[:, NH + s - 8, :], work[:, 9 - s, :], ACT.Copy)
                        if s in (12, 14):
                            h = s // 2 - 6
                            read_proj(b, 3 + h, uza[:, h, :], work[:, 1, :], ACT.Identity,
                                      bias=cols[:, CBC + h:CBC + h + 1])
                        if s == 15:
                            act.wait_ge(pa_read, NPA * b + 5)
                            act.activation(uza[:, :, :], uza[:, :, :], ACT.Silu).then_inc(silu_done, 1)
                            act.preload_act_table_set(EXP_LN_TABLES)
                        if s == 17:
                            reach(act, (xd_stored, 16 * (it + 1)))
                            read_proj(b, 5, xd[:, :], work[0:NX, 1, :], ACT.Copy)
                        for h, s0, s1, s2 in ((0, 19, 20, 22), (1, 21, 23, 25)):
                            c = 6 * b
                            if s == s0:
                                pairs = NP // NH * (h + 1)
                                for r in range(RING):
                                    n = 32 * ((NP // RING) * it + pairs // RING)
                                    reach(act, (du_spread[r], n), (delta_spread[r], n))
                                bias = cols[:, DTC + h:DTC + h + 1]
                                act.wait_ge(pa_filled, NPA * b + 7 + h)
                                act.activation(delta[:, h, :], work[:, h, :], ACT.Abs, bias=bias)
                                read_proj(b, 6 + h, du[:, h, :], work[:, h, :], ACT.Relu, bias=bias)
                                act.wait_ge(pa_read, NPA * b + 7 + h)
                                act.activation(delta[:, h, :], delta[:, h, :], ACT.Exp, scale=-1.0).then_inc(soft[h], 1)
                            if s == s1:
                                act.wait_ge(soft[h], c + 1)
                                act.activation(sp1[:, h, :], delta[:, h, :], ACT.Ln, bias=csts[:, 1:2]).then_inc(soft[h], 1)
                                act.wait_ge(soft[h], c + 2)
                                act.activation(sp1[:, h, :], sp1[:, h, :], ACT.Exp, scale=-1.0).then_inc(soft[h], 1)
                            if s == s2:
                                act.wait_ge(lp_ready, 3 * (NH * b + h) + 1)
                                act.activation(delta[:, h, :], sp1[:, h, :], ACT.Square).then_inc(soft[h], 1)
                                act.wait_ge(soft[h], c + 4)
                                act.activation(sp2[:, h, :], delta[:, h, :], ACT.Square, bias=csts[:, 2:3]).then_inc(soft[h], 1)
                                act.wait_ge(soft[h], c + 5)
                                act.activation(sp2[:, h, :], sp2[:, h, :], ACT.Square, bias=csts[:, 3:4],
                                               scale=L1P_K).then_inc(soft[h], 1)

            over_batches(act, iteration)

        @block.tensor
        def _(pe):
            pe.wait_ge(rows_loaded, 7 * 16)
            pe.wait_ge(const_made, 6)
            pe.transpose(work[:, 0, 0:NROW], rows[0:NROW, :], ident[0:NROW, 0:NROW]).then_inc(cols_turned, 1)

            def sum_states(it, j):
                pe.wait_ge(hc_done, NP * it + j + 1)
                if 2 * j % (NG // NH) == 0:
                    h = 2 * j // (NG // NH)
                    reach(pe, (y_skip, NH * (it - 1) + h + 1))
                for i in range(2):
                    g = 2 * j + i
                    strip = 32 * ((g // GQ) % (P // 32))
                    last = pe.matmul(ypsum[strip:strip + 32, g * CG // P, :], sel[:, g % GQ, :],
                                     uring[:, j % RING, i, :], start=(g % GQ == 0), stop=(g % GQ == GQ - 1),
                                     tile_position=(0, strip))
                last.then_inc(summed, 1)

            def proj(b, k, products):
                for n, (o, w, r) in enumerate(products):
                    last = pe.matmul(o, w, r, start=(n == 0), stop=(n == len(products) - 1))
                last.then_inc(pa_filled, 1)

            def split_product(o, weights, moving):
                pe.matmul(o, weights[0], moving[0], start=True, stop=False)
                pe.matmul(o, weights[1], moving[0], start=False, stop=False)
                return pe.matmul(o, weights[0], moving[1], start=False, stop=True)

            def ffn(b, k):
                if k < UN:
                    e, f = k // FC, k % FC
                    if k == 0:
                        if isinstance(b, int) and b == 0:
                            pe.wait_ge(low_made, 2)
                        pe.wait_ge(xfl_ready, b + 1)
                    reach(pe, (relu_done, UN * b + k - 1))
                    last = split_product(hpsum[:, k % 2, :], (w1h[:, e, f * P:(f + 1) * P], w1l[:, e, f * P:(f + 1) * P]),
                                         (xfh[:, :], xfl[:, :]))
                    last.then_inc(h_filled, 1)
                if k >= LAG:
                    e, i = (k - LAG) // FC, (k - LAG) % FC
                    pe.wait_ge(relu_done, UN * b + FC * (e + 1))
                    if i == 0:
                        reach(pe, (acc_done, E * b + e - 1))
                    for f in range(FC):
                        last = pe.matmul(opsum[:, e % 2, i * P:(i + 1) * P], hb[:, e % 2, f, i * P:(i + 1) * P],
                                         w2[:, e, f, :], start=(f == 0), stop=(f == FC - 1))
                    last.then_inc(o_filled, 1)

            def iteration(it, ahead, scan, post, late):
                for s in range(SS):
                    if post and s in (0, 2):
                        sum_states(it - 1, NP - 2 + s // 2)
                    if scan and s >= 4 and s % 2 == 0:
                        sum_states(it, s // 2 - 2)
                    if late:
                        for k in old_units(s):
                            ffn(it - 2, k)
                    if ahead and s == 5:
                        pe.wait_ge(xn_ready, it + 2)
                        reach(pe, (pa_read, NPA * (it + 1)))
                        for i in range(NT):
                            last = pe.transpose(work[:, 1, i * P:(i + 1) * P], xn[:, i, :], ident[:, :])
                        last.then_inc(pa_filled, 1)
                    if post:
                        b = it - 1
                        if s == 5:
                            if isinstance(it, int) and it == 1:
                                pe.wait_ge(ffn_loaded, 16 * (3 + E))
                            pe.wait_ge(gated, NH * (b + 1))
                            pe.wait_ge(pa_read, NPA * (it + 1) if scan else NPA * NBATCH)
                            for i in range(NT):
                                for h in range(NH):
                                    last = pe.matmul(work[:, 0, i * P:(i + 1) * P], yg[:, h, i * P:(i + 1) * P],
                                                     wout[:, h, :], start=(h == 0), stop=(h == NH - 1))
                            last.then_inc(pc_filled, 1)
                        if s == 9:
                            reach(pe, (pa_read, NPA * (it + 1) + 2 if ahead else 0))
                            pe.wait_ge(xf_ready, b + 1)
                            for i in range(NT):
                                last = pe.transpose(work[:, 1, i * P:(i + 1) * P], r1[:, i, :], ident[:, :])
                            last.then_inc(pc_filled, 1)
                        if s == 10:
                            if isinstance(it, int) and it == 1:
                                pe.wait_ge(low_made, 1)
                            reach(pe, (pa_read, NPA * (it + 1) + 3 if ahead else 0))
                            pe.wait_ge(xfl_ready, b + 1)
                            pe.wait_ge(r1_ready, b + 1)
                            for i in range(NT):
                                last = split_product(work[:, 0, i * E:(i + 1) * E],
                                                     (xfh[:, i * P:(i + 1) * P], xfl[:, i * P:(i + 1) * P]),
                                                     (wrh[:, :], wrl[:, :]))
                            last.then_inc(pc_filled, 1)
                        for k in new_units(s):
                            ffn(b, k)
                        if s == 14:
                            pe.wait_ge(w_ready, b + 1)
                            for i in range(NT):
                                last = pe.transpose(work[0:E, 0, i * P:(i + 1) * P], wr[:, i, :], ident[:, :])
                            last.then_inc(pc_filled, 1)
                        if s == 15:
                            pe.wait_ge(wrT_ready, b + 1)
                            for i in range(NT):
                                last = pe.matmul(work[:, 0, i * P:(i + 1) * P], wrT[:, i * P:(i + 1) * P],
                                                 b2s[:, :], start=True, stop=True)
                            last.then_inc(pc_filled, 1)
                    if ahead:
                        b = it + 1
                        if s == 7:
                            pe.wait_ge(pa_read, NPA * b + 1)
                            if isinstance(it, int) and it < 0:
                                pe.wait_ge(w_folded, 1)
                                pe.wait_ge(cols_copied, 1)
                        if s == 8:
                            reach(pe, (r1_ready, it))
                        if s in (7, 8):
                            h = s - 7
                            proj(b, 1 + h, [(work[:, 1 - h, :], wz[:, h * P:(h + 1) * P], xnT[:, TAPS - 1:])])
                        if s in (11, 13):
                            h = s // 2 - 5
                            if h == 0:
                                reach(pe, (xfl_ready, it))
                            pe.wait_ge(pa_read, NPA * b + 3 + h)
                            proj(b, 3 + h, [(work[:, 1, :], wconv[:, k, h * P:(h + 1) * P], xnT[:, k:k + T])
                                            for k in range(TAPS)])
                        if s == 16:
                            pe.wait_ge(silu_done, b + 1)
                            for c0 in range(0, NX, 32):
                                c1 = min(c0 + 32, NX)
                                for h in range(NH):
                                    last = pe.matmul(work[c0:c1, 1, :], wxp[:, h, c0:c1], uza[:, h, :], start=(h == 0),
                                                     stop=(h == NH - 1), tile_position=(0, c0))
                            last.then_inc(pa_filled, 1)
                        if s == 18:
                            pe.wait_ge(pa_read, NPA * b + 6)
                            reach(pe, (b2_added, it))
                            for h in range(NH):
                                proj(b, 6 + h, [(work[:, h, :], wdt[:, h * P:(h + 1) * P], xd[0:RANK, :])])

            over_batches(pe, iteration)

        @block.vector
        def _(dve):
            for k, c in enumerate((EPS, 2.0, L1P_A, L1P_KB)):
                dve.memset(csts[:, k:k + 1], c)
            dve.memset(xnT[:, 0:TAPS - 1], 0.0).then_inc(pads_made, 1)
            dve.wait_ge(const_made, 3)
            dve.tensor_copy(iota_f[:, :], iota_i[:, :]).then_inc(pads_made, 1)
            dve.wait_ge(proj_loaded, 5 * 16)
            for k in range(TAPS):
                last = dve.tensor_tensor(wconv[:, k, :], win_raw, conv_raw.rearrange("p (c k) -> p k c", k=TAPS)[:, k, :],
                                  ALU.mult)
            last.then_inc(w_folded, 1)
            dve.wait_ge(a_exp, 1)
            dve.tensor_scalar(Amat[:, :], Amat[:, :], -1.0, None, ALU.mult).then_inc(a_made, 1)

            def token_stats(src, st_, mv_, steps, base):
                for i in range(NT):
                    last = dve.bn_stats(st_[:, i, :], src[:, i, :])
                last.then_inc(steps, 1)
                dve.wait_ge(steps, base + 1)
                dve.memset(fence[:, :], 0.0)
                for i in range(NT):
                    last = dve.bn_aggr(mv_[:, i, :], st_[:, i, :])
                last.then_inc(steps, 1)

            def normalize(dst, src, mv_, rs_):
                for i in range(NT):
                    last = dve.tensor_scalar(dst[:, i, :], src[:, i, :], mv_[:, i, 0:1], rs_[:, i:i + 1],
                                             ALU.subtract, ALU.mult)
                return last

            def stats_ahead(b):
                dve.wait_ge(x_loaded, 16 * (b + 1))
                token_stats(xa, st, mv, norm_a, 4 * b)

            def layernorms_ahead(b):
                dve.wait_ge(rs_ready, 4 * b + 2)
                reach(dve, (xh_stored, 16 * b))
                reach(dve, (xn_ready, b))
                normalize(xha, xa, mv, rs).then_inc(xh_ready, 1)
                dve.tensor_tensor(rq[:, 0, :], mv[:, :, 1], rs[:, :], ALU.mult).then_inc(norm_a, 1)
                dve.wait_ge(norm_a, 4 * b + 3)
                dve.tensor_tensor(rq[:, 1, :], rq[:, 0, :], rs[:, :], ALU.mult).then_inc(norm_a, 1)

            def log1p_argument(b, h):
                dve.wait_ge(soft[h], 6 * b + 3)
                dve.tensor_tensor(sp1[:, h, :], sp1[:, h, :], delta[:, h, :], ALU.mult).then_inc(lp_ready, 1)

            def step_size(b, h):
                c = 3 * (NH * b + h)
                dve.wait_ge(soft[h], 6 * b + 6)
                dve.scalar_tensor_tensor(out=sp2[:, h, :], in0=delta[:, h, :], scalar=L1P_D, in1=sp2[:, h, :],
                                         op0=ALU.mult, op1=ALU.add).then_inc(lp_ready, 1)
                dve.wait_ge(lp_ready, c + 2)
                dve.scalar_tensor_tensor(out=sp2[:, h, :], in0=sp2[:, h, :], scalar=L1P_E, in1=sp1[:, h, :],
                                         op0=ALU.add, op1=ALU.mult).then_inc(lp_ready, 1)
                dve.wait_ge(lp_ready, c + 3)
                dve.scalar_tensor_tensor(out=delta[:, h, :], in0=sp2[:, h, :], scalar=2.0, in1=du[:, h, :],
                                         op0=ALU.mult, op1=ALU.add).then_inc(delta_ready, 1)

            def drive(it, j):
                if j == 0:
                    dve.wait_ge(b_loaded, 16 * (it + 1))
                dve.wait_ge(du_spread[j % RING], 32 * ((NP // RING) * it + j // RING + 1))
                v = uring[:, j % RING, :, :]
                bb = bcc[:, 0, :].unsqueeze(1).broadcast_to([P, 2, T])
                dve.tensor_tensor(v, v, bb, ALU.mult).then_inc(db_done, 1)

            def scan_group(it, g):
                j, i = g // 2, g % 2
                if i == 0:
                    dve.wait_ge(db_done, NP * it + j + 1)
                dve.wait_ge(exp_done, NG * it + g + 1)
                v = uring[:, j % RING, i, :]
                ins = dve.tensor_tensor_scan(v, dring[:, j % RING, i, :], v, 0.0, ALU.mult, ALU.add)
                if i == 1:
                    ins.then_inc(scan_done, 1)

            def skip(b, h):
                if h == 0:
                    dve.wait_ge(uz_copied, 16 * (b + 1))
                    reach(dve, (pc_filled, NPC * (b - 1) + 1))
                dve.wait_ge(summed, NP * b + NP // NH * (h + 1))
                dve.scalar_tensor_tensor(out=yg[:, h, :], in0=uzc[:, h, :], scalar=cols[:, DSC + h:DSC + h + 1],
                                         in1=ypsum[:, h, :], op0=ALU.mult, op1=ALU.add).then_inc(y_skip, 1)

            def residual(b):
                dve.wait_ge(pc_filled, NPC * b + 1)
                dve.wait_ge(xc_loaded, 32 * (b + 1))
                dve.tensor_tensor(r1[:, :, :], work[:, 0, :].rearrange("p (i d) -> p i d", d=D), xhc[:, :, :],
                                  ALU.add).then_inc(r1_ready, 1)
                dve.wait_ge(r1_ready, b + 1)
                token_stats(r1, stc, mvc, norm_c, 5 * b)

            def residual_normed(b):
                dve.wait_ge(rsc_ready, 4 * b + 2)
                normalize(r1, r1, mvc, rsc).then_inc(norm_c, 1)
                dve.wait_ge(norm_c, 5 * b + 3)
                reach(dve, (x1_copied, 16 * b))
                dve.tensor_tensor(x1[:, :, :], r1[:, :, :], xc[:, :, :], ALU.add).then_inc(x1_ready, 1)
                dve.wait_ge(x1_ready, b + 1)
                token_stats(x1, stc, mvc, norm_c, 5 * b + 3)

            def experts_input(b):
                dve.wait_ge(rsc_ready, 4 * b + 4)
                normalize(r1, x1, mvc, rsc).then_inc(xf_ready, 1)

            def experts_input_low(b):
                dve.wait_ge(xfh_ready, b + 1)
                dve.tensor_tensor(xfl[:, :], work[:, 1, :], xfh[:, :].bitcast(F32), ALU.subtract).then_inc(xfl_ready, 1)

            def top_two(b):
                dve.wait_ge(pc_filled, NPC * b + 3)
                dve.tensor_tensor(lg[:, :, :], work[:, 0, 0:NT * E].rearrange("p (i e) -> p i e", e=E),
                                  brb[:, :].unsqueeze(1).broadcast_to([P, NT, E]), ALU.add).then_inc(route, 1)
                dve.wait_ge(route, RT * b + 1)
                dve.memset(fence[:, :], 0.0)
                for i in range(NT):
                    last = dve.max(mx[:, i, :], lg[:, i, :])
                last.then_inc(route, 1)
                dve.wait_ge(route, RT * b + 2)
                dve.tensor_tensor(ex[:, :, :], lg[:, :, :], mx[:, :, 0:1].broadcast_to([P, NT, E]),
                                  ALU.subtract).then_inc(route, 1)
                for i in range(NT):
                    last = dve.max_index(ix[:, i, :], mx[:, i, :], lg[:, i, :])
                last.then_inc(route, 1)
                dve.wait_ge(route, RT * b + 4)
                dve.tensor_copy(ixf[:, :, :], ix[:, :, 0:2]).then_inc(route, 1)
                dve.wait_ge(route, RT * b + 5)
                numbers = iota_f[:, :].unsqueeze(1).broadcast_to([P, NT, E])
                dve.tensor_tensor(m1[:, :, :], numbers, ixf[:, :, 0:1].broadcast_to([P, NT, E]), ALU.is_equal)
                dve.tensor_tensor(m2[:, :, :], numbers, ixf[:, :, 1:2].broadcast_to([P, NT, E]), ALU.is_equal
                                  ).then_inc(route, 1)
                dve.wait_ge(route, RT * b + 6)
                dve.tensor_tensor(m1[:, :, :], m1[:, :, :], m2[:, :, :], ALU.add).then_inc(route, 1)

            def softmax(b):
                dve.wait_ge(route_exp, b + 1)
                dve.wait_ge(route, RT * b + 7)
                dve.tensor_tensor(ex[:, :, :], ex[:, :, :], m1[:, :, :], ALU.mult).then_inc(route, 1)
                dve.wait_ge(route, RT * b + 8)
                dve.tensor_reduce(sm[:, :], ex[:, :, :], AX.X, ALU.add).then_inc(route, 1)
                dve.wait_ge(route, RT * b + 9)
                dve.reciprocal(sm[:, :], sm[:, :]).then_inc(route, 1)
                dve.wait_ge(route, RT * b + 10)
                dve.tensor_tensor(wr[:, :, :], ex[:, :, :], sm[:, :].unsqueeze(2).broadcast_to([P, NT, E]),
                                  ALU.mult).then_inc(w_ready, 1)

            def start_sum(b):
                dve.wait_ge(pc_filled, NPC * b + 5)
                dve.tensor_copy(acc[:, :, :], work[:, 0, :].rearrange("p (i d) -> p i d", d=D)).then_inc(b2_added, 1)

            def add_expert(b, e):
                dve.wait_ge(o_filled, UN * b + FC * (e + 1))
                if e == 0:
                    dve.wait_ge(b2_added, b + 1)
                else:
                    dve.wait_ge(acc_done, E * b + e)
                for i in range(NT):
                    last = dve.scalar_tensor_tensor(out=acc[:, i, :], in0=opsum[:, e % 2, i * P:(i + 1) * P],
                                                    scalar=wr[:, i, e:e + 1], in1=acc[:, i, :],
                                                    op0=ALU.mult, op1=ALU.add)
                last.then_inc(acc_done, 1)

            def output(b):
                dve.wait_ge(acc_done, E * (b + 1))
                token_stats(acc, sto, mvo, norm_o, 3 * b)

            def output_normed(b):
                dve.wait_ge(rso_ready, 2 * b + 2)
                reach(dve, (pa_filled, NPA * (b + 3) + 1 if not isinstance(b, int) or b + 3 < NBATCH else 0))
                dve.wait_ge(x1_copied, 16 * (b + 1))
                normalize(xo, acc, mvo, rso).then_inc(norm_o, 1)
                dve.wait_ge(norm_o, 3 * b + 3)
                dve.tensor_tensor(xo[:, :, :], xo[:, :, :], x1e[:, :, :], ALU.add).then_inc(out_ready, 1)

            def iteration(it, ahead, scan, post, late):
                for s in range(SS):
                    if scan and s % 2 == 0:
                        drive(it, s // 2)
                    if scan:
                        scan_group(it, s)
                    if late:
                        if s in (2, 4, 7, 11):
                            add_expert(it - 2, E - FC + (2, 4, 7, 11).index(s))
                        if s == 12:
                            output(it - 2)
                        if s == 13:
                            output_normed(it - 2)
                    if post:
                        if s == 3:
                            skip(it - 1, 1)
                        if s == 6:
                            residual(it - 1)
                        if s == 7:
                            residual_normed(it - 1)
                        if s == 8:
                            experts_input(it - 1)
                        if s == 10:
                            experts_input_low(it - 1)
                        if s == 11:
                            if isinstance(it, int) and it == 1:
                                dve.wait_ge(pads_made, 2)
                                dve.wait_ge(ffn_loaded, 16 * (3 + E))
                            top_two(it - 1)
                        if s == 13:
                            softmax(it - 1)
                        if s == 17:
                            start_sum(it - 1)
                        if s in (18, 22, 26, 30):
                            add_expert(it - 1, (s - 18) // 4)
                    if ahead and s in (21, 24):
                        log1p_argument(it + 1, (s - 21) // 3)
                    if ahead and s in (23, 26):
                        step_size(it + 1, (s - 23) // 3)
                    if ahead and s == 1:
                        stats_ahead(it + 1)
                    if ahead and s == 3:
                        layernorms_ahead(it + 1)
                    if scan and s == 19:
                        skip(it, 0)

            over_batches(dve, iteration)


_INS = ['x', 'ln_g', 'ln_b', 'W_in', 'conv_w', 'conv_b', 'W_xp', 'W_dt', 'dt_bias', 'A_log', 'D_skip', 'W_out']
_FFN = ['W_router', 'b_router', 'W1', 'b1', 'W2', 'b2']


def kernel(**inputs):
    import numpy as _np
    import concourse.bacc as _bacc
    from concourse import mybir as _mybir
    from concourse.bass_utils import run_bass_kernel_spmd as _run

    nc = _bacc.Bacc("TRN2", target_bir_lowering=False, num_devices=1)
    arrays, args = {}, []
    for name in [f"L0_attn_{n}" for n in _INS] + [f"L0_ffn_{n}" for n in _FFN]:
        a = _np.ascontiguousarray(inputs[name])
        arrays[f"in_{name}"] = a
        args.append(nc.dram_tensor(f"in_{name}", a.shape, _mybir.dt.from_np(a.dtype), kind="ExternalInput").ap())
    shape = inputs["L0_attn_x"].shape
    args.append(nc.dram_tensor("out_x", shape, _mybir.dt.float32, kind="ExternalOutput").ap())
    mamba_moe_kernel(nc, *args)
    r = _run(nc, [arrays], core_ids=[0])
    return r.results[0]["out_x"]
```

```python
from contextlib import ExitStack

import concourse.bass as bass
from concourse import mybir

F32 = mybir.dt.float32
F32R = mybir.dt.float32r
U32 = mybir.dt.uint32
I32 = mybir.dt.int32
ALU = mybir.AluOpType
ACT = mybir.ActivationFunctionType
AX = mybir.AxisListType

P = 128
EPS = 1e-5
L1P_A, L1P_K, L1P_KB = 0.24810788804420705, 0.3753309023989405, 0.19728378793895784
L1P_D, L1P_E = 0.25123911755073414, 0.9514290285127261
EXP_LN_TABLES = "natural_log_exp_and_others"

AT = dict(
    stats_a=0, act_rs=3, norm_a=3, act_rs2=3, act_xn=5, pe_turn_a=6, act_turn_a=8,
    pe_z=(7, 8), act_z=(8, 9), pe_u=(13, 15), act_u=(13, 16), act_silu=16, pe_xp=18, act_xp=18, pe_dt=19,
    act_soft=(19, 21), act_log=(19, 23), log1p=(21, 25), act_square=(21, 25), step_size=(23, 27),
    pool_du=(23, 29),
    skip=(17, 4), pool_gate=(21, 3), sum_last=(0, 4),
    pe_out=5, residual=7, act_rsc=(6, 8), normed=8, x_in=9, pe_turn_c=9, act_turn_c=8, x_low=11,
    pe_router=11, top_two=12, act_route=13, softmax=13, pe_wr=15, act_wr=15, pe_b2=16, start_sum=18,
    add_new=(20, 24, 27, 31),
    add_old=(3, 6, 9, 12), stats_o=13, act_rso=14, out=14,
    lead=3,
    new=(0, 2, 4, 5, 6, 7, 8, 9, 10, 11, 12, 13, 14, 15, 16, 17, 18, 19, 20, 21, 22),
    old=(22, 24, 25, 26, 27, 28, 30, 31, 33, 35, 36, 37, 37),
)


def reach(eng, *waits):
    waits = [(sem, count) for sem, count in waits if not (isinstance(count, int) and count <= 0)]
    for _, count in waits:
        if not isinstance(count, int):
            eng.compute_val(count)
    for sem, count in waits:
        eng.wait_ge(sem, count)


def mamba_moe_kernel(nc, x, ln_g, ln_b, W_in, conv_w, conv_b, W_xp, W_dt, dt_bias, A_log, D_skip,
                     W_out, W_router, b_router, W1, b1, W2, b2, out):
    NBATCH, T, D = x.shape
    DI = D_skip.shape[0]
    NST = A_log.shape[1]
    TAPS = conv_w.shape[2]
    RANK = W_dt.shape[0]
    E, _, DF = W1.shape
    assert D == P and T == 512 and DI == 2 * P and E == 8 and P % NST == 0
    NT = T // P
    NH = DI // P
    CG = P // NST
    NG = DI // CG
    NP = NG // 2
    GQ = 32 // CG
    FC = DF // P
    UN = E * FC
    LAG = 5
    RING, PRE = 8, 4
    SS = NG
    LEAD = AT["lead"]
    RT = 10
    NPA, NPC = 8, 5

    ctx = ExitStack()
    with ctx:
        def sb(name, shape, dt=F32):
            return ctx.enter_context(nc.sbuf_tensor(name, shape, dt))

        def ps(name, shape):
            return ctx.enter_context(nc.psum_tensor(name, shape, F32))

        def sem(name):
            return ctx.enter_context(nc.semaphore(name))

        NROW = NG + UN + 3 * NH + 2
        rows = sb("rows", [P, P])
        cols = sb("cols", [P, NROW])
        Amat = sb("Amat", [P, NG])
        wz = sb("wz", [P, DI])
        wconv = sb("wconv", [P, TAPS, DI])
        wxp = sb("wxp", [P, NH, RANK + 2 * NST])
        wdt = sb("wdt", [RANK, DI])
        wout = sb("wout", [P, NH, D])
        wrt = sb("wrt", [P, E])
        wrh, wrl = sb("wrh", [P, E], F32R), sb("wrl", [P, E], F32R)
        w1h, w1l = sb("w1h", [P, E, DF], F32R), sb("w1l", [P, E, DF], F32R)
        xfh, xfl = sb("xfh", [P, T], F32R), sb("xfl", [P, T], F32R)
        brb = sb("brb", [P, E])
        w2 = sb("w2", [P, E, FC, D])
        b2s = sb("b2s", [E, D])
        ident = sb("ident", [P, P])
        sel = sb("sel", [P, GQ, 32])
        iota_i = sb("iota_i", [P, E], I32)
        iota_f = sb("iota_f", [P, E])
        B1C = NG
        CBC, DTC, DSC, GC, BC = (B1C + UN + k for k in (0, NH, 2 * NH, 3 * NH, 3 * NH + 1))

        xa = sb("xa", [P, NT, D])
        xha = sb("xha", [P, NT, D])
        xnT = sb("xnT", [P, TAPS - 1 + T])
        uza = sb("uza", [P, 2 * NH, T])
        NX = RANK + 2 * NST
        xd = sb("xd", [NX, T])
        delta = sb("delta", [P, NH, T])
        du = sb("du", [P, NH, T])
        st = sb("st", [P, NT, 6])
        mv = sb("mv", [P, NT, 2])
        rs = sb("rs", [P, NT])
        rq = sb("rq", [P, 2, NT])
        rs2 = sb("rs2", [P, NT])
        bcc = sb("bcc", [P, 2, T])
        dring = sb("dring", [P, RING, 2, T])
        uring = sb("uring", [P, RING, 2, T])
        assert E * DF == (RING - PRE) * 2 * T and TAPS * DI <= 2 * T and DI <= T
        w1_raw = dring[:, PRE:, :, :].rearrange("p r i t -> p (r i t)").rearrange("p (e n) -> p e n", e=E)
        conv_raw = uring[:, PRE, :, :].rearrange("p i t -> p (i t)")[:, 0:TAPS * DI]
        win_raw = uring[:, PRE + 1, 0, 0:DI]
        uzc = sb("uzc", [P, 2 * NH, T])
        xc = sb("xc", [P, NT, D])
        xhc = sb("xhc", [P, NT, D])
        yg = sb("yg", [P, NH, T])
        r1 = sb("r1", [P, NT, D])
        x1 = sb("x1", [P, NT, D])
        stc = sb("stc", [P, NT, 6])
        mvc = sb("mvc", [P, NT, 2])
        rsc = sb("rsc", [P, NT])
        sto = sb("sto", [P, NT, 6])
        mvo = sb("mvo", [P, NT, 2])
        rso = sb("rso", [P, NT])
        fence = sb("fence", [P, 1])
        csts = sb("csts", [P, 4])
        sp1 = sb("sp1", [P, NH, T])
        sp2 = sb("sp2", [P, NH, T])
        lg = sb("lg", [P, NT, E])
        mx = sb("mx", [P, NT, E])
        ix = sb("ix", [P, NT, E], U32)
        ixf = sb("ixf", [P, NT, 2])
        m1 = sb("m1", [P, NT, E])
        m2 = sb("m2", [P, NT, E])
        ex = sb("ex", [P, NT, E])
        sm = sb("sm", [P, NT])
        wr = sb("wr", [P, NT, E])
        wrT = sb("wrT", [E, T])
        hb = sb("hb", [P, 2, FC, T])
        acc = sb("acc", [P, NT, D])
        x1e = sb("x1e", [P, NT, D])
        xo = sb("xo", [P, NT, D])
        xn = xo

        xd_dram = nc.dram_tensor("xd_dram", [NBATCH, NX, T], F32, kind="Internal").ap()
        xh_dram = nc.dram_tensor("xh_dram", [NBATCH, P, NT * D], F32, kind="Internal").ap()

        ypsum = ps("ypsum", [P, NH, T])
        hpsum = ps("hpsum", [P, 2, T])
        opsum = ps("opsum", [P, 2, T])
        work = ps("work", [P, 2, T])

        rows_loaded, proj_loaded, ffn_loaded = sem("rows_loaded"), sem("proj_loaded"), sem("ffn_loaded")
        w1_loaded, high_made, low_made = sem("w1_loaded"), sem("high_made"), sem("low_made")
        const_made, cols_turned, cols_copied, a_exp = (sem("const_made"), sem("cols_turned"),
                                                       sem("cols_copied"), sem("a_exp"))
        a_made, w_folded, pads_made = sem("a_made"), sem("w_folded"), sem("pads_made")
        x_loaded, xc_loaded, uz_copied = sem("x_loaded"), sem("xc_loaded"), sem("uz_copied")
        b_loaded, c_loaded, x1_copied = sem("b_loaded"), sem("c_loaded"), sem("x1_copied")
        xd_stored, xh_stored = sem("xd_stored"), sem("xh_stored")
        out_stored = sem("out_stored")
        delta_spread = [sem(f"delta_spread{r}") for r in range(RING)]
        du_spread = [sem(f"du_spread{r}") for r in range(RING)]
        norm_a, xh_ready = sem("norm_a"), sem("xh_ready")
        db_done, scan_done, y_skip = sem("db_done"), sem("scan_done"), sem("y_skip")
        norm_c, r1_ready, x1_ready, xf_ready = (sem("norm_c"), sem("r1_ready"), sem("x1_ready"),
                                                sem("xf_ready"))
        route, w_ready, b2_added = sem("route"), sem("w_ready"), sem("b2_added")
        acc_done, norm_o, out_ready = sem("acc_done"), sem("norm_o"), sem("out_ready")
        rs_ready, rsc_ready, rso_ready = sem("rs_ready"), sem("rsc_ready"), sem("rso_ready")
        xn_ready, pa_read, silu_done = sem("xn_ready"), sem("pa_read"), sem("silu_done")
        lp_ready = sem("lp_ready")
        soft, exp_done = [sem(f"soft{h}") for h in range(NH)], sem("exp_done")
        xfh_ready, xfl_ready, route_exp, wrT_ready = sem("xfh_ready"), sem("xfl_ready"), sem("route_exp"), sem("wrT_ready")
        relu_done = sem("relu_done")
        hc_done, delta_ready, du_ready, gated = (sem("hc_done"), sem("delta_ready"), sem("du_ready"),
                                                 sem("gated"))
        summed, pa_filled, pc_filled = sem("summed"), sem("pa_filled"), sem("pc_filled")
        h_filled, o_filled = sem("h_filled"), sem("o_filled")

        def over_batches(eng, iteration, looped=NBATCH - 1):
            def flags(it):
                return dict(ahead=it + 1 < NBATCH, scan=0 <= it < NBATCH, post=0 <= it - 1 < NBATCH,
                            late=0 <= it - 2 < NBATCH)
            for it in (-1, 0, 1):
                iteration(it, **flags(it))
            with eng.Fori(2, looped) as it:
                iteration(it, ahead=True, scan=True, post=True, late=True)
            for it in range(looped, NBATCH + 2):
                iteration(it, **flags(it))

        def new_units(s):
            cut = AT["new"]
            n = s - (SS + 1 - len(cut))
            return list(range(cut[n], cut[n + 1])) if n >= 0 else []

        def old_units(s):
            cut = AT["old"]
            return list(range(cut[s], cut[s + 1])) if s + 1 < len(cut) else []
        assert AT["new"][-1] == AT["old"][0] and AT["old"][-1] == UN + LAG

        block = ctx.enter_context(nc.Block())

        @block.sync
        def _(sp):
            sp.dma_start(xa[:, :, :], x[0].rearrange("(i p) d -> p i d", p=P)).then_inc(x_loaded, 16)
            sp.dma_start(rows[0:NG, :], A_log.rearrange("(g c) n -> g (c n)", c=CG)).then_inc(rows_loaded, 16)
            sp.dma_start(rows[B1C:B1C + UN, :], b1.rearrange("e (f p) -> (e f) p", p=P)).then_inc(rows_loaded, 16)
            for at, v in ((CBC, conv_b), (DTC, dt_bias), (DSC, D_skip), (GC, ln_g), (BC, ln_b)):
                k = v.shape[0] // P
                sp.dma_start(rows[at:at + k, :], v.rearrange("(h p) -> h p", p=P)).then_inc(rows_loaded, 16)
            sp.dma_start(win_raw, W_in[:, 0:DI]).then_inc(proj_loaded, 16)
            sp.dma_start(wz[:, :], W_in[:, DI:2 * DI]).then_inc(proj_loaded, 16)
            sp.dma_start(conv_raw, conv_w.rearrange("c a k -> (c a k)").partition_broadcast(P)).then_inc(proj_loaded, 16)
            sp.dma_start(wxp[:, :, :], W_xp.rearrange("(h p) n -> p h n", p=P)).then_inc(proj_loaded, 16)
            sp.dma_start(wdt[:, :], W_dt).then_inc(proj_loaded, 16)
            sp.dma_start(w1_raw, W1.rearrange("e d n -> d e n")).then_inc(w1_loaded, 16)
            sp.dma_start(wrt[:, :], W_router).then_inc(w1_loaded, 16)
            sp.dma_start(wout[:, :, :], W_out.rearrange("(h p) n -> p h n", p=P)).then_inc(ffn_loaded, 16)
            sp.dma_start(brb[:, :], b_router.partition_broadcast(P)).then_inc(ffn_loaded, 16)
            sp.dma_start(b2s[:, :], b2).then_inc(ffn_loaded, 16)
            for e in range(E):
                sp.dma_start(w2[:, e, :, :], W2[e].rearrange("(f p) n -> p f n", p=P)).then_inc(ffn_loaded, 16)

            def spread(it, j):
                pair = NP * it + j
                made = [(du_ready, NH * it + j // (NP // NH) + 1)] if j % (NP // NH) == 0 else []
                reach(sp, *made, (summed, pair - RING + 1))
                for i in range(2):
                    g = 2 * j + i
                    c0 = (g * CG) % P
                    for src, ring, n, loaded in ((delta, dring, RING, delta_spread), (du, uring, RING, du_spread)):
                        rowsrc = src[c0:c0 + CG, g * CG // P, :].unsqueeze(1).broadcast_to([CG, NST, T])
                        sp.dma_start(ring[:, j % n, i, :], rowsrc).then_inc(loaded[j % n], 16)

            def load_b_c(b):
                for k, (used, loaded) in enumerate(((db_done, b_loaded), (hc_done, c_loaded))):
                    reach(sp, *([] if k else [(xd_stored, 16 * (b + 1))]), (used, NP * b))
                    n0 = RANK + k * NST
                    sp.dma_start(bcc[:, k, :], xd_dram[bass.ds(b, 1), n0:n0 + NST, :].broadcast_to([CG, NST, T])
                                 ).then_inc(loaded, 16)

            def iteration(it, ahead, scan, post, late):
                if scan:
                    if not (isinstance(it, int) and it == 0):
                        load_b_c(it)
                    if isinstance(it, int) and it == 0:
                        sp.wait_ge(low_made, 2)
                        sp.wait_ge(w_folded, 1)
                    spread(it, 4)
                    spread(it, 5)
                    reach(sp, (gated, NH * it))
                    sp.dma_start(uzc[:, :, :], uza[:, :, :]).then_inc(uz_copied, 16)
                if ahead:
                    sp.wait_ge(xh_ready, it + 2)
                    sp.dma_start(xh_dram[bass.ds(it + 1, 1)].rearrange("a p n -> p (a n)"),
                                 xha[:, :, :].rearrange("p i d -> p (i d)")).then_inc(xh_stored, 16)
                    if not (isinstance(it, int) and it + 2 >= NBATCH):
                        sp.dma_start(xa[:, :, :], x[bass.ds(it + 2, 1)].rearrange("a (i p) d -> p (a i) d", p=P)
                                     ).then_inc(x_loaded, 16)
                if scan:
                    spread(it, 6)
                    spread(it, 7)
                    reach(sp, (x1_ready, it))
                    sp.wait_ge(xh_stored, 16 * (it + 1))
                    sp.dma_start(xc[:, :, :], x[bass.ds(it, 1)].rearrange("a (i p) d -> p (a i) d", p=P)
                                 ).then_inc(xc_loaded, 16)
                    sp.dma_start(xhc[:, :, :].rearrange("p i d -> p (i d)"),
                                 xh_dram[bass.ds(it, 1)].rearrange("a p n -> p (a n)")).then_inc(xc_loaded, 16)
                    for j in range(8, 11):
                        spread(it, j)
                if late:
                    sp.wait_ge(out_ready, it - 1)
                    sp.dma_start(out[bass.ds(it - 2, 1)].rearrange("a (i p) d -> p (a i) d", p=P), xo[:, :, :]
                                 ).then_inc(out_stored, 16)
                    sp.wait_ge(out_stored, 16 * (it - 1))
                if post:
                    sp.wait_ge(x1_ready, it)
                    sp.dma_start(x1e[:, :, :], x1[:, :, :]).then_inc(x1_copied, 16)
                if scan:
                    for j in range(11, NP):
                        spread(it, j)
                if ahead:
                    sp.wait_ge(pa_read, NPA * (it + 1) + 6)
                    sp.dma_start(xd_dram[bass.ds(it + 1, 1)].rearrange("a n t -> n (a t)"), xd[:, :]).then_inc(xd_stored, 16)
                    if isinstance(it, int) and it < 0:
                        load_b_c(0)
                    for j in range(PRE):
                        spread(it + 1, j)

            over_batches(sp, iteration, looped=NBATCH - 2)
            sp.wait_ge(out_stored, 16 * NBATCH)
            sp.wait_ge(xd_stored, 16 * NBATCH)
            sp.wait_ge(xh_stored, 16 * NBATCH)

        @block.gpsimd
        def _(pool):
            pool.memset(ident[:, :], 0.0).then_inc(const_made, 1)
            pool.memset(sel[:, :, :], 1.0).then_inc(const_made, 1)
            pool.iota(iota_i[:, :], [[1, E]], base=0, channel_multiplier=0).then_inc(const_made, 1)
            pool.wait_ge(const_made, 3)
            pool.affine_select(out=ident[:, :], in_=ident[:, :], compare_op=ALU.not_equal, fill=1.0, base=0,
                               pattern=[[-1, P]], channel_multiplier=1).then_inc(const_made, 1)
            pool.affine_select(out=sel[:, :, :], in_=sel[:, :, :], compare_op=ALU.is_ge, fill=0.0, base=0,
                               pattern=[[P, GQ], [-NST, 32]], channel_multiplier=1).then_inc(const_made, 1)
            pool.wait_ge(const_made, 5)
            pool.affine_select(out=sel[:, :, :], in_=sel[:, :, :], compare_op=ALU.is_ge, fill=0.0, base=NST - 1,
                               pattern=[[-P, GQ], [NST, 32]], channel_multiplier=-1).then_inc(const_made, 1)

            def states_to_output(it, j):
                if j == 0:
                    pool.wait_ge(c_loaded, 16 * (it + 1))
                pool.wait_ge(scan_done, NP * it + j + 1)
                h = uring[:, j % RING, :, :]
                c = bcc[:, 1, :].unsqueeze(1).broadcast_to([P, 2, T])
                pool.tensor_tensor(h, h, c, ALU.mult).then_inc(hc_done, 1)

            def gate(b, h):
                pool.wait_ge(y_skip, NH * b + h + 1)
                pool.tensor_tensor(yg[:, h, :], yg[:, h, :], uzc[:, NH + h, :], ALU.mult).then_inc(gated, 1)

            def steps_of_time(b, h):
                pool.wait_ge(delta_ready, NH * b + h + 1)
                pool.wait_ge(silu_done, b + 1)
                pool.tensor_tensor(du[:, h, :], delta[:, h, :], uza[:, h, :], ALU.mult).then_inc(du_ready, 1)

            def iteration(it, ahead, scan, post, late):
                for s in range(SS):
                    if s == 0 and post:
                        states_to_output(it - 1, NP - 1)
                    if s == AT["pool_gate"][1] and post:
                        gate(it - 1, 1)
                    if s >= 2 and s % 2 == 0 and scan:
                        states_to_output(it, s // 2 - 1)
                    if s == AT["pool_gate"][0] and scan:
                        gate(it, 0)
                    if s == 0 and isinstance(it, int) and it < 0:
                        pool.wait_ge(high_made, 2)
                        pool.tensor_tensor(wrl[:, :], wrt[:, :], wrh[:, :].bitcast(F32), ALU.subtract).then_inc(low_made, 1)
                        pool.tensor_tensor(w1l[:, :, :], w1_raw, w1h[:, :, :].bitcast(F32), ALU.subtract).then_inc(low_made, 1)
                    if s in AT["pool_du"] and ahead:
                        steps_of_time(it + 1, AT["pool_du"].index(s))

            over_batches(pool, iteration)

        @block.scalar
        def _(act):
            act.preload_act_table_set(EXP_LN_TABLES)
            act.wait_ge(cols_turned, 1)
            act.activation(cols[:, :], work[:, 0, 0:NROW], ACT.Copy).then_inc(cols_copied, 1)
            act.wait_ge(cols_copied, 1)
            act.activation(Amat[:, :], cols[:, 0:NG], ACT.Exp).then_inc(a_exp, 1)

            def decay(it, g):
                j, i = g // 2, g % 2
                if isinstance(it, int) and it == 0 and g == 0:
                    act.wait_ge(a_made, 1)
                if i == 0:
                    act.wait_ge(delta_spread[j % RING], 32 * ((NP // RING) * it + j // RING + 1))
                act.activation(dring[:, j % RING, i, :], dring[:, j % RING, i, :], ACT.Exp,
                               scale=Amat[:, g:g + 1]).then_inc(exp_done, 1)

            def read_proj(b, k, dst, src, func, **affine):
                act.wait_ge(pa_filled, NPA * b + k + 1)
                act.activation(dst, src, func, **affine).then_inc(pa_read, 1)

            def relu(b, u):
                e, f = u // FC, u % FC
                act.wait_ge(h_filled, UN * b + u + 1)
                if f == 0:
                    reach(act, (o_filled, UN * b + FC * (e - 1)))
                act.activation(hb[:, e % 2, f, :], hpsum[:, u % 2, :], ACT.Relu,
                               bias=cols[:, B1C + u:B1C + u + 1]).then_inc(relu_done, 1)

            def inverse_deviation(dst, var, ready, count):
                act.activation(dst[:, :], var, ACT.Ln, bias=csts[:, 0:1]).then_inc(ready, 1)
                act.wait_ge(ready, count - 1)
                act.activation(dst[:, :], dst[:, :], ACT.Exp, scale=-0.5).then_inc(ready, 1)

            def iteration(it, ahead, scan, post, late):
                for s in range(SS):
                    if scan and s + LEAD < NG:
                        decay(it, s + LEAD)
                    if ahead and s + LEAD >= NG:
                        decay(it + 1, s + LEAD - NG)
                    if ahead and s == AT["act_turn_a"]:
                        read_proj(it + 1, 0, xnT[:, TAPS - 1:], work[:, 1, :], ACT.Identity,
                                  scale=cols[:, GC:GC + 1], bias=cols[:, BC:BC + 1])
                    if ahead and s in AT["act_z"]:
                        h = AT["act_z"].index(s)
                        if h == 0:
                            reach(act, (uz_copied, 16 * (it + 1)))
                        read_proj(it + 1, 1 + h, uza[:, NH + h, :], work[:, 1 - h, :], ACT.Copy)
                    if s == 11 and isinstance(it, int) and it < 0:
                        act.wait_ge(w1_loaded, 32)
                        act.activation(wrh[:, :], wrt[:, :], ACT.Copy).then_inc(high_made, 1)
                        act.activation(w1h[:, :, :], w1_raw, ACT.Copy).then_inc(high_made, 1)
                    if late and s == AT["act_rso"]:
                        act.wait_ge(norm_o, 3 * (it - 2) + 2)
                        inverse_deviation(rso, mvo[:, :, 1], rso_ready, 2 * (it - 2) + 2)
                    if post:
                        b = it - 1
                        for k in range(2):
                            if s == AT["act_rsc"][k]:
                                act.wait_ge(norm_c, 5 * b + (2, 5)[k])
                                inverse_deviation(rsc, mvc[:, :, 1], rsc_ready, 4 * b + 2 * (k + 1))
                        if s == AT["act_turn_c"]:
                            act.wait_ge(pc_filled, NPC * b + 2)
                            act.activation(xfh[:, :], work[:, 1, :], ACT.Copy).then_inc(xfh_ready, 1)
                        if s == AT["act_route"]:
                            act.wait_ge(route, RT * b + 3)
                            act.activation(ex[:, :, :], ex[:, :, :], ACT.Exp).then_inc(route_exp, 1)
                    if late:
                        for k in old_units(s):
                            if k < UN:
                                relu(it - 2, k)
                    if post:
                        for k in new_units(s):
                            relu(b, k)
                        if s == AT["act_wr"]:
                            act.wait_ge(pc_filled, NPC * b + 4)
                            act.activation(wrT[:, :], work[0:E, 0, :], ACT.Copy).then_inc(wrT_ready, 1)
                    if ahead:
                        b = it + 1
                        if s == AT["act_rs"]:
                            if isinstance(it, int) and it < 0:
                                act.wait_ge(pads_made, 1)
                            act.wait_ge(norm_a, 4 * b + 2)
                            inverse_deviation(rs, mv[:, :, 1], rs_ready, 4 * b + 2)
                        if s == AT["act_rs2"]:
                            act.wait_ge(norm_a, 4 * b + 4)
                            inverse_deviation(rs2, rq[:, 1, :], rs_ready, 4 * b + 4)
                        if s == AT["act_xn"]:
                            act.wait_ge(rs_ready, 4 * b + 4)
                            act.wait_ge(xh_ready, b + 1)
                            reach(act, (x1_copied, 16 * (it - 1)))
                            for i in range(NT):
                                last = act.activation(xn[:, i, :], xha[:, i, :], ACT.Copy, scale=rs2[:, i:i + 1])
                            last.then_inc(xn_ready, 1)
                        if s in AT["act_u"]:
                            h = AT["act_u"].index(s)
                            read_proj(b, 3 + h, uza[:, h, :], work[:, 1, :], ACT.Identity,
                                      bias=cols[:, CBC + h:CBC + h + 1])
                        if s == AT["act_silu"]:
                            act.wait_ge(pa_read, NPA * b + 5)
                            act.activation(uza[:, :, :], uza[:, :, :], ACT.Silu).then_inc(silu_done, 1)
                            act.preload_act_table_set(EXP_LN_TABLES)
                        if s == AT["act_xp"]:
                            reach(act, (xd_stored, 16 * (it + 1)))
                            read_proj(b, 5, xd[:, :], work[0:NX, 1, :], ACT.Copy)
                        c = 6 * b
                        for h in range(NH):
                            if s == AT["act_soft"][h]:
                                pairs = NP // NH * (h + 1)
                                for r in range(RING):
                                    n = 32 * ((NP // RING) * it + pairs // RING)
                                    reach(act, (du_spread[r], n), (delta_spread[r], n))
                                bias = cols[:, DTC + h:DTC + h + 1]
                                act.wait_ge(pa_filled, NPA * b + 7 + h)
                                act.activation(delta[:, h, :], work[:, h, :], ACT.Abs, bias=bias)
                                read_proj(b, 6 + h, du[:, h, :], work[:, h, :], ACT.Relu, bias=bias)
                                act.wait_ge(pa_read, NPA * b + 7 + h)
                                act.activation(delta[:, h, :], delta[:, h, :], ACT.Exp, scale=-1.0).then_inc(soft[h], 1)
                            if s == AT["act_log"][h]:
                                act.wait_ge(soft[h], c + 1)
                                act.activation(sp1[:, h, :], delta[:, h, :], ACT.Ln, bias=csts[:, 1:2]).then_inc(soft[h], 1)
                                act.wait_ge(soft[h], c + 2)
                                act.activation(sp1[:, h, :], sp1[:, h, :], ACT.Exp, scale=-1.0).then_inc(soft[h], 1)
                            if s == AT["act_square"][h]:
                                act.wait_ge(lp_ready, 3 * (NH * b + h) + 1)
                                act.activation(delta[:, h, :], sp1[:, h, :], ACT.Square).then_inc(soft[h], 1)
                                act.wait_ge(soft[h], c + 4)
                                act.activation(sp2[:, h, :], delta[:, h, :], ACT.Square, bias=csts[:, 2:3]).then_inc(soft[h], 1)
                                act.wait_ge(soft[h], c + 5)
                                act.activation(sp2[:, h, :], sp2[:, h, :], ACT.Square, bias=csts[:, 3:4],
                                               scale=L1P_K).then_inc(soft[h], 1)

            over_batches(act, iteration)

        @block.tensor
        def _(pe):
            pe.wait_ge(rows_loaded, 7 * 16)
            pe.wait_ge(const_made, 6)
            pe.transpose(work[:, 0, 0:NROW], rows[0:NROW, :], ident[0:NROW, 0:NROW]).then_inc(cols_turned, 1)

            def sum_states(it, j):
                pe.wait_ge(hc_done, NP * it + j + 1)
                if 2 * j % (NG // NH) == 0:
                    h = 2 * j // (NG // NH)
                    reach(pe, (y_skip, NH * (it - 1) + h + 1))
                for i in range(2):
                    g = 2 * j + i
                    strip = 32 * ((g // GQ) % (P // 32))
                    last = pe.matmul(ypsum[strip:strip + 32, g * CG // P, :], sel[:, g % GQ, :],
                                     uring[:, j % RING, i, :], start=(g % GQ == 0), stop=(g % GQ == GQ - 1),
                                     tile_position=(0, strip))
                last.then_inc(summed, 1)

            def proj(b, k, products):
                for n, (o, w, r) in enumerate(products):
                    last = pe.matmul(o, w, r, start=(n == 0), stop=(n == len(products) - 1))
                last.then_inc(pa_filled, 1)

            def split_product(o, weights, moving):
                pe.matmul(o, weights[0], moving[0], start=True, stop=False)
                pe.matmul(o, weights[1], moving[0], start=False, stop=False)
                return pe.matmul(o, weights[0], moving[1], start=False, stop=True)

            def ffn(b, k):
                if k < UN:
                    e, f = k // FC, k % FC
                    if k == 0:
                        if isinstance(b, int) and b == 0:
                            pe.wait_ge(low_made, 2)
                        pe.wait_ge(xfl_ready, b + 1)
                    reach(pe, (relu_done, UN * b + k - 1))
                    last = split_product(hpsum[:, k % 2, :], (w1h[:, e, f * P:(f + 1) * P], w1l[:, e, f * P:(f + 1) * P]),
                                         (xfh[:, :], xfl[:, :]))
                    last.then_inc(h_filled, 1)
                if k >= LAG:
                    e, i = (k - LAG) // FC, (k - LAG) % FC
                    pe.wait_ge(relu_done, UN * b + FC * (e + 1))
                    if i == 0:
                        reach(pe, (acc_done, E * b + e - 1))
                    for f in range(FC):
                        last = pe.matmul(opsum[:, e % 2, i * P:(i + 1) * P], hb[:, e % 2, f, i * P:(i + 1) * P],
                                         w2[:, e, f, :], start=(f == 0), stop=(f == FC - 1))
                    last.then_inc(o_filled, 1)

            def iteration(it, ahead, scan, post, late):
                for s in range(SS):
                    if post and s in AT["sum_last"]:
                        sum_states(it - 1, NP - 2 + AT["sum_last"].index(s))
                    if scan and s >= 4 and s % 2 == 0:
                        sum_states(it, s // 2 - 2)
                    if late:
                        for k in old_units(s):
                            ffn(it - 2, k)
                    if ahead and s == AT["pe_turn_a"]:
                        pe.wait_ge(xn_ready, it + 2)
                        reach(pe, (pa_read, NPA * (it + 1)))
                        for i in range(NT):
                            last = pe.transpose(work[:, 1, i * P:(i + 1) * P], xn[:, i, :], ident[:, :])
                        last.then_inc(pa_filled, 1)
                    if post:
                        b = it - 1
                        if s == AT["pe_out"]:
                            if isinstance(it, int) and it == 1:
                                pe.wait_ge(ffn_loaded, 16 * (3 + E))
                            pe.wait_ge(gated, NH * (b + 1))
                            pe.wait_ge(pa_read, NPA * (it + 1) if scan else NPA * NBATCH)
                            for i in range(NT):
                                for h in range(NH):
                                    last = pe.matmul(work[:, 0, i * P:(i + 1) * P], yg[:, h, i * P:(i + 1) * P],
                                                     wout[:, h, :], start=(h == 0), stop=(h == NH - 1))
                            last.then_inc(pc_filled, 1)
                        if s == AT["pe_turn_c"]:
                            reach(pe, (pa_read, NPA * (it + 1) + 2 if ahead else 0))
                            pe.wait_ge(xf_ready, b + 1)
                            for i in range(NT):
                                last = pe.transpose(work[:, 1, i * P:(i + 1) * P], r1[:, i, :], ident[:, :])
                            last.then_inc(pc_filled, 1)
                        if s == AT["pe_router"]:
                            if isinstance(it, int) and it == 1:
                                pe.wait_ge(low_made, 1)
                            reach(pe, (pa_read, NPA * (it + 1) + 3 if ahead else 0))
                            pe.wait_ge(xfl_ready, b + 1)
                            pe.wait_ge(r1_ready, b + 1)
                            for i in range(NT):
                                last = split_product(work[:, 0, i * E:(i + 1) * E],
                                                     (xfh[:, i * P:(i + 1) * P], xfl[:, i * P:(i + 1) * P]),
                                                     (wrh[:, :], wrl[:, :]))
                            last.then_inc(pc_filled, 1)
                        for k in new_units(s):
                            ffn(b, k)
                        if s == AT["pe_wr"]:
                            pe.wait_ge(w_ready, b + 1)
                            for i in range(NT):
                                last = pe.transpose(work[0:E, 0, i * P:(i + 1) * P], wr[:, i, :], ident[:, :])
                            last.then_inc(pc_filled, 1)
                        if s == AT["pe_b2"]:
                            pe.wait_ge(wrT_ready, b + 1)
                            for i in range(NT):
                                last = pe.matmul(work[:, 0, i * P:(i + 1) * P], wrT[:, i * P:(i + 1) * P],
                                                 b2s[:, :], start=True, stop=True)
                            last.then_inc(pc_filled, 1)
                    if ahead:
                        b = it + 1
                        if s == AT["pe_z"][0]:
                            pe.wait_ge(pa_read, NPA * b + 1)
                            if isinstance(it, int) and it < 0:
                                pe.wait_ge(w_folded, 1)
                                pe.wait_ge(cols_copied, 1)
                        if s == AT["pe_z"][1]:
                            reach(pe, (r1_ready, it))
                        if s in AT["pe_z"]:
                            h = AT["pe_z"].index(s)
                            proj(b, 1 + h, [(work[:, 1 - h, :], wz[:, h * P:(h + 1) * P], xnT[:, TAPS - 1:])])
                        if s in AT["pe_u"]:
                            h = AT["pe_u"].index(s)
                            if h == 0:
                                reach(pe, (xfl_ready, it))
                            pe.wait_ge(pa_read, NPA * b + 3 + h)
                            proj(b, 3 + h, [(work[:, 1, :], wconv[:, k, h * P:(h + 1) * P], xnT[:, k:k + T])
                                            for k in range(TAPS)])
                        if s == AT["pe_xp"]:
                            pe.wait_ge(silu_done, b + 1)
                            for c0 in range(0, NX, 32):
                                c1 = min(c0 + 32, NX)
                                for h in range(NH):
                                    last = pe.matmul(work[c0:c1, 1, :], wxp[:, h, c0:c1], uza[:, h, :], start=(h == 0),
                                                     stop=(h == NH - 1), tile_position=(0, c0))
                            last.then_inc(pa_filled, 1)
                        if s == AT["pe_dt"]:
                            pe.wait_ge(pa_read, NPA * b + 6)
                            reach(pe, (b2_added, it))
                            for h in range(NH):
                                proj(b, 6 + h, [(work[:, h, :], wdt[:, h * P:(h + 1) * P], xd[0:RANK, :])])

            over_batches(pe, iteration)

        @block.vector
        def _(dve):
            for k, c in enumerate((EPS, 2.0, L1P_A, L1P_KB)):
                dve.memset(csts[:, k:k + 1], c)
            dve.memset(xnT[:, 0:TAPS - 1], 0.0).then_inc(pads_made, 1)
            dve.wait_ge(const_made, 3)
            dve.tensor_copy(iota_f[:, :], iota_i[:, :]).then_inc(pads_made, 1)

            def prepare_weights():
                dve.wait_ge(proj_loaded, 5 * 16)
                for k in range(TAPS):
                    taps = conv_raw.rearrange("p (c k) -> p k c", k=TAPS)[:, k, :]
                    last = dve.tensor_tensor(wconv[:, k, :], win_raw, taps, ALU.mult)
                last.then_inc(w_folded, 1)
                dve.wait_ge(a_exp, 1)
                dve.tensor_scalar(Amat[:, :], Amat[:, :], -1.0, None, ALU.mult).then_inc(a_made, 1)

            def token_stats(src, st_, mv_, steps, base):
                for i in range(NT):
                    last = dve.bn_stats(st_[:, i, :], src[:, i, :])
                last.then_inc(steps, 1)
                dve.wait_ge(steps, base + 1)
                dve.memset(fence[:, :], 0.0)
                for i in range(NT):
                    last = dve.bn_aggr(mv_[:, i, :], st_[:, i, :])
                last.then_inc(steps, 1)

            def normalize(dst, src, mv_, rs_):
                for i in range(NT):
                    last = dve.tensor_scalar(dst[:, i, :], src[:, i, :], mv_[:, i, 0:1], rs_[:, i:i + 1],
                                             ALU.subtract, ALU.mult)
                return last

            def stats_ahead(b):
                dve.wait_ge(x_loaded, 16 * (b + 1))
                token_stats(xa, st, mv, norm_a, 4 * b)

            def layernorms_ahead(b):
                dve.wait_ge(rs_ready, 4 * b + 2)
                reach(dve, (xh_stored, 16 * b))
                reach(dve, (xn_ready, b))
                normalize(xha, xa, mv, rs).then_inc(xh_ready, 1)
                dve.tensor_tensor(rq[:, 0, :], mv[:, :, 1], rs[:, :], ALU.mult).then_inc(norm_a, 1)
                dve.wait_ge(norm_a, 4 * b + 3)
                dve.tensor_tensor(rq[:, 1, :], rq[:, 0, :], rs[:, :], ALU.mult).then_inc(norm_a, 1)

            def log1p_argument(b, h):
                dve.wait_ge(soft[h], 6 * b + 3)
                dve.tensor_tensor(sp1[:, h, :], sp1[:, h, :], delta[:, h, :], ALU.mult).then_inc(lp_ready, 1)

            def step_size(b, h):
                c = 3 * (NH * b + h)
                dve.wait_ge(soft[h], 6 * b + 6)
                dve.scalar_tensor_tensor(out=sp2[:, h, :], in0=delta[:, h, :], scalar=L1P_D, in1=sp2[:, h, :],
                                         op0=ALU.mult, op1=ALU.add).then_inc(lp_ready, 1)
                dve.wait_ge(lp_ready, c + 2)
                dve.scalar_tensor_tensor(out=sp2[:, h, :], in0=sp2[:, h, :], scalar=L1P_E, in1=sp1[:, h, :],
                                         op0=ALU.add, op1=ALU.mult).then_inc(lp_ready, 1)
                dve.wait_ge(lp_ready, c + 3)
                dve.scalar_tensor_tensor(out=delta[:, h, :], in0=sp2[:, h, :], scalar=2.0, in1=du[:, h, :],
                                         op0=ALU.mult, op1=ALU.add).then_inc(delta_ready, 1)

            def drive(it, j):
                if j == 0:
                    dve.wait_ge(b_loaded, 16 * (it + 1))
                dve.wait_ge(du_spread[j % RING], 32 * ((NP // RING) * it + j // RING + 1))
                v = uring[:, j % RING, :, :]
                bb = bcc[:, 0, :].unsqueeze(1).broadcast_to([P, 2, T])
                dve.tensor_tensor(v, v, bb, ALU.mult).then_inc(db_done, 1)

            def scan_group(it, g):
                j, i = g // 2, g % 2
                if i == 0:
                    dve.wait_ge(db_done, NP * it + j + 1)
                dve.wait_ge(exp_done, NG * it + g + 1)
                v = uring[:, j % RING, i, :]
                ins = dve.tensor_tensor_scan(v, dring[:, j % RING, i, :], v, 0.0, ALU.mult, ALU.add)
                if i == 1:
                    ins.then_inc(scan_done, 1)

            def skip(b, h):
                if h == 0:
                    dve.wait_ge(uz_copied, 16 * (b + 1))
                    reach(dve, (pc_filled, NPC * (b - 1) + 1))
                dve.wait_ge(summed, NP * b + NP // NH * (h + 1))
                dve.scalar_tensor_tensor(out=yg[:, h, :], in0=uzc[:, h, :], scalar=cols[:, DSC + h:DSC + h + 1],
                                         in1=ypsum[:, h, :], op0=ALU.mult, op1=ALU.add).then_inc(y_skip, 1)

            def residual(b):
                dve.wait_ge(pc_filled, NPC * b + 1)
                dve.wait_ge(xc_loaded, 32 * (b + 1))
                dve.tensor_tensor(r1[:, :, :], work[:, 0, :].rearrange("p (i d) -> p i d", d=D), xhc[:, :, :],
                                  ALU.add).then_inc(r1_ready, 1)
                dve.wait_ge(r1_ready, b + 1)
                token_stats(r1, stc, mvc, norm_c, 5 * b)

            def residual_normed(b):
                dve.wait_ge(rsc_ready, 4 * b + 2)
                normalize(r1, r1, mvc, rsc).then_inc(norm_c, 1)
                dve.wait_ge(norm_c, 5 * b + 3)
                reach(dve, (x1_copied, 16 * b))
                dve.tensor_tensor(x1[:, :, :], r1[:, :, :], xc[:, :, :], ALU.add).then_inc(x1_ready, 1)
                dve.wait_ge(x1_ready, b + 1)
                token_stats(x1, stc, mvc, norm_c, 5 * b + 3)

            def experts_input(b):
                dve.wait_ge(rsc_ready, 4 * b + 4)
                normalize(r1, x1, mvc, rsc).then_inc(xf_ready, 1)

            def experts_input_low(b):
                dve.wait_ge(xfh_ready, b + 1)
                dve.tensor_tensor(xfl[:, :], work[:, 1, :], xfh[:, :].bitcast(F32), ALU.subtract).then_inc(xfl_ready, 1)

            def top_two(b):
                dve.wait_ge(pc_filled, NPC * b + 3)
                dve.tensor_tensor(lg[:, :, :], work[:, 0, 0:NT * E].rearrange("p (i e) -> p i e", e=E),
                                  brb[:, :].unsqueeze(1).broadcast_to([P, NT, E]), ALU.add).then_inc(route, 1)
                dve.wait_ge(route, RT * b + 1)
                dve.memset(fence[:, :], 0.0)
                for i in range(NT):
                    last = dve.max(mx[:, i, :], lg[:, i, :])
                last.then_inc(route, 1)
                dve.wait_ge(route, RT * b + 2)
                dve.tensor_tensor(ex[:, :, :], lg[:, :, :], mx[:, :, 0:1].broadcast_to([P, NT, E]),
                                  ALU.subtract).then_inc(route, 1)
                for i in range(NT):
                    last = dve.max_index(ix[:, i, :], mx[:, i, :], lg[:, i, :])
                last.then_inc(route, 1)
                dve.wait_ge(route, RT * b + 4)
                dve.tensor_copy(ixf[:, :, :], ix[:, :, 0:2]).then_inc(route, 1)
                dve.wait_ge(route, RT * b + 5)
                numbers = iota_f[:, :].unsqueeze(1).broadcast_to([P, NT, E])
                dve.tensor_tensor(m1[:, :, :], numbers, ixf[:, :, 0:1].broadcast_to([P, NT, E]), ALU.is_equal)
                dve.tensor_tensor(m2[:, :, :], numbers, ixf[:, :, 1:2].broadcast_to([P, NT, E]), ALU.is_equal
                                  ).then_inc(route, 1)
                dve.wait_ge(route, RT * b + 6)
                dve.tensor_tensor(m1[:, :, :], m1[:, :, :], m2[:, :, :], ALU.add).then_inc(route, 1)

            def softmax(b):
                dve.wait_ge(route_exp, b + 1)
                dve.wait_ge(route, RT * b + 7)
                dve.tensor_tensor(ex[:, :, :], ex[:, :, :], m1[:, :, :], ALU.mult).then_inc(route, 1)
                dve.wait_ge(route, RT * b + 8)
                dve.tensor_reduce(sm[:, :], ex[:, :, :], AX.X, ALU.add).then_inc(route, 1)
                dve.wait_ge(route, RT * b + 9)
                dve.reciprocal(sm[:, :], sm[:, :]).then_inc(route, 1)
                dve.wait_ge(route, RT * b + 10)
                dve.tensor_tensor(wr[:, :, :], ex[:, :, :], sm[:, :].unsqueeze(2).broadcast_to([P, NT, E]),
                                  ALU.mult).then_inc(w_ready, 1)

            def start_sum(b):
                dve.wait_ge(pc_filled, NPC * b + 5)
                dve.tensor_copy(acc[:, :, :], work[:, 0, :].rearrange("p (i d) -> p i d", d=D)).then_inc(b2_added, 1)

            def add_expert(b, e):
                dve.wait_ge(o_filled, UN * b + FC * (e + 1))
                if e == 0:
                    dve.wait_ge(b2_added, b + 1)
                else:
                    dve.wait_ge(acc_done, E * b + e)
                for i in range(NT):
                    last = dve.scalar_tensor_tensor(out=acc[:, i, :], in0=opsum[:, e % 2, i * P:(i + 1) * P],
                                                    scalar=wr[:, i, e:e + 1], in1=acc[:, i, :],
                                                    op0=ALU.mult, op1=ALU.add)
                last.then_inc(acc_done, 1)

            def output(b):
                dve.wait_ge(acc_done, E * (b + 1))
                token_stats(acc, sto, mvo, norm_o, 3 * b)

            def output_normed(b):
                dve.wait_ge(rso_ready, 2 * b + 2)
                reach(dve, (pa_filled, NPA * (b + 3) + 1 if not isinstance(b, int) or b + 3 < NBATCH else 0))
                dve.wait_ge(x1_copied, 16 * (b + 1))
                normalize(xo, acc, mvo, rso).then_inc(norm_o, 1)
                dve.wait_ge(norm_o, 3 * b + 3)
                dve.tensor_tensor(xo[:, :, :], xo[:, :, :], x1e[:, :, :], ALU.add).then_inc(out_ready, 1)

            def iteration(it, ahead, scan, post, late):
                for s in range(SS):
                    if scan and s % 2 == 0:
                        drive(it, s // 2)
                    if scan:
                        scan_group(it, s)
                    if late:
                        if s in AT["add_old"]:
                            add_expert(it - 2, len(AT["add_new"]) + AT["add_old"].index(s))
                        if s == AT["stats_o"]:
                            output(it - 2)
                        if s == AT["out"]:
                            output_normed(it - 2)
                    if post:
                        if s == AT["skip"][1]:
                            skip(it - 1, 1)
                        if s == AT["residual"]:
                            residual(it - 1)
                        if s == AT["normed"]:
                            residual_normed(it - 1)
                        if s == AT["x_in"]:
                            experts_input(it - 1)
                        if s == AT["x_low"]:
                            experts_input_low(it - 1)
                        if s == AT["top_two"]:
                            if isinstance(it, int) and it == 1:
                                dve.wait_ge(pads_made, 2)
                                dve.wait_ge(ffn_loaded, 16 * (3 + E))
                            top_two(it - 1)
                        if s == AT["softmax"]:
                            softmax(it - 1)
                        if s == AT["start_sum"]:
                            start_sum(it - 1)
                        if s in AT["add_new"]:
                            add_expert(it - 1, AT["add_new"].index(s))
                    if ahead:
                        if s == AT["stats_a"]:
                            stats_ahead(it + 1)
                        if s == AT["norm_a"]:
                            layernorms_ahead(it + 1)
                            if isinstance(it, int) and it < 0:
                                prepare_weights()
                        if s in AT["log1p"]:
                            log1p_argument(it + 1, AT["log1p"].index(s))
                        if s in AT["step_size"]:
                            step_size(it + 1, AT["step_size"].index(s))
                    if scan and s == AT["skip"][0]:
                        skip(it, 0)

            over_batches(dve, iteration)


_INS = ['x', 'ln_g', 'ln_b', 'W_in', 'conv_w', 'conv_b', 'W_xp', 'W_dt', 'dt_bias', 'A_log', 'D_skip', 'W_out']
_FFN = ['W_router', 'b_router', 'W1', 'b1', 'W2', 'b2']


def kernel(**inputs):
    import numpy as _np
    import concourse.bacc as _bacc
    from concourse import mybir as _mybir
    from concourse.bass_utils import run_bass_kernel_spmd as _run

    nc = _bacc.Bacc("TRN2", target_bir_lowering=False, num_devices=1)
    arrays, args = {}, []
    for name in [f"L0_attn_{n}" for n in _INS] + [f"L0_ffn_{n}" for n in _FFN]:
        a = _np.ascontiguousarray(inputs[name])
        arrays[f"in_{name}"] = a
        args.append(nc.dram_tensor(f"in_{name}", a.shape, _mybir.dt.from_np(a.dtype), kind="ExternalInput").ap())
    shape = inputs["L0_attn_x"].shape
    args.append(nc.dram_tensor("out_x", shape, _mybir.dt.float32, kind="ExternalOutput").ap())
    mamba_moe_kernel(nc, *args)
    r = _run(nc, [arrays], core_ids=[0])
    return r.results[0]["out_x"]
```
